# Optimizing a Trainium2 kernel written in Bass

```python
import numpy as np
import jax
import jax.numpy as jnp

def _softmax(x, axis=-1):
    return jax.nn.softmax(x, axis=axis)

def _gelu(x):
    return jax.nn.gelu(x, approximate=True)

def _silu(x):
    return jax.nn.silu(x)

def _sigmoid(x):
    return jax.nn.sigmoid(x)

def _layernorm(x, axis=-1, eps=1e-05):
    m = jnp.mean(x, axis=axis, keepdims=True)
    v = jnp.var(x, axis=axis, keepdims=True)
    return (x - m) / jnp.sqrt(v + eps)

def _scatter_add(tgt, idx, src, axis=0):
    return tgt.at[idx].add(src)

def _segment_sum(src, seg, n):
    return jax.ops.segment_sum(src, seg, n)
kernel_name = 'mk_lm_tower_d1_tok_ids512_r4_4409b7'

def setup_inputs(seed: int=0):
    np.random.seed(seed)
    _w = jnp.asarray

    def _rec_inputs():
        import jax
        import jax.numpy as jnp
        _rk = jax.random.key(seed)
        x = jax.random.randint(jax.random.fold_in(_rk, 1), (16, 128), 0, 12564, jnp.int32)
        return x
    x = _rec_inputs()

    def _L0_tok_setup():
        import jax, jax.numpy as jnp
        import numpy as np
        VOCAB = 50257
        EMBED = 128
        key = jax.random.key(seed)
        k1, k2 = jax.random.split(key)
        x = jax.random.randint(k1, (8, 512), 0, VOCAB, dtype=jnp.int64 if jax.config.jax_enable_x64 else jnp.int32)
        w = jax.random.normal(k2, (VOCAB, EMBED), dtype=jnp.float32)
        return {'x': x, 'w': w}
    _L0_tok_all = _L0_tok_setup()
    _L0_tok_in = {k: v for k, v in _L0_tok_all.items() if k in ('w',)}
    del _L0_tok_all

    def _L0_attn_setup():
        import jax, jax.numpy as jnp
        import numpy as np
        B, N, IN_F, OUT_F, HEAD_D = (4, 1024, 128, 128, 64)
        THRESHOLD_LAMBDA_MIN = 0.001
        key = jax.random.key(seed)
        kx, kq, kk, kv = jax.random.split(key, 4)
        x = jax.random.normal(kx, (B, N, IN_F), dtype=jnp.float32)
        s = 1.0 / np.sqrt(IN_F)
        Wq = jax.random.uniform(kq, (HEAD_D, IN_F), dtype=jnp.float32, minval=-s, maxval=s)
        Wk = jax.random.uniform(kk, (HEAD_D, IN_F), dtype=jnp.float32, minval=-s, maxval=s)
        Wv = jax.random.uniform(kv, (OUT_F, IN_F), dtype=jnp.float32, minval=-s, maxval=s)
        log_lambda = jnp.zeros((1,), dtype=jnp.float32)
        return {'x': x, 'Wq': Wq, 'Wk': Wk, 'Wv': Wv, 'log_lambda': log_lambda}
    _L0_attn_all = _L0_attn_setup()
    _L0_attn_in = {k: v for k, v in _L0_attn_all.items() if k in ('Wq', 'Wk', 'Wv', 'log_lambda')}
    del _L0_attn_all

    def _L0_ffn_setup():
        import jax, jax.numpy as jnp
        import numpy as np
        DIM, DEPTH, MULT = (128, 3, 4)
        E = 2 ** DEPTH
        HID = MULT * DIM
        B, S = (4, 256)

        def _leaf_probs(flat_x, rw, rb):
            n_tok = flat_x.shape[0]
            leaf = jnp.ones((n_tok, 1), dtype=flat_x.dtype)
            for d in range(DEPTH):
                off, n = (2 ** d - 1, 2 ** d)
                logits = flat_x @ rw[off:off + n].T + rb[off:off + n]
                p = jax.nn.sigmoid(logits)
                leaf = (leaf[:, :, None] * jnp.stack([1.0 - p, p], axis=2)).reshape(n_tok, 2 * n)
            return leaf
        key = jax.random.key(seed)
        ks = jax.random.split(key, 7)
        sd = 1.0 / np.sqrt(DIM)
        sh = 1.0 / np.sqrt(HID)
        return {'x': jax.random.normal(ks[0], (B, S, DIM), dtype=jnp.float32), 'rw': jax.random.normal(ks[1], (E - 1, DIM), dtype=jnp.float32) * sd, 'rb': jax.random.normal(ks[2], (E - 1,), dtype=jnp.float32) * sd, 'w1': jax.random.normal(ks[3], (E, DIM, HID), dtype=jnp.float32) * sd, 'b1': jax.random.normal(ks[4], (E, HID), dtype=jnp.float32) * sd, 'w2': jax.random.normal(ks[5], (E, HID, DIM), dtype=jnp.float32) * sh, 'b2': jax.random.normal(ks[6], (E, DIM), dtype=jnp.float32) * sh}
    _L0_ffn_all = _L0_ffn_setup()
    _L0_ffn_in = {k: v for k, v in _L0_ffn_all.items() if k in ('rw', 'rb', 'w1', 'b1', 'w2', 'b2')}
    del _L0_ffn_all
    return {'x': x, 'L0_tok_w': _L0_tok_in['w'], 'L0_attn_Wq': _L0_attn_in['Wq'], 'L0_attn_Wk': _L0_attn_in['Wk'], 'L0_attn_Wv': _L0_attn_in['Wv'], 'L0_attn_log_lambda': _L0_attn_in['log_lambda'], 'L0_ffn_rw': _L0_ffn_in['rw'], 'L0_ffn_rb': _L0_ffn_in['rb'], 'L0_ffn_w1': _L0_ffn_in['w1'], 'L0_ffn_b1': _L0_ffn_in['b1'], 'L0_ffn_w2': _L0_ffn_in['w2'], 'L0_ffn_b2': _L0_ffn_in['b2']}

def reference(x, L0_tok_w, L0_attn_Wq, L0_attn_Wk, L0_attn_Wv, L0_attn_log_lambda, L0_ffn_rw, L0_ffn_rb, L0_ffn_w1, L0_ffn_b1, L0_ffn_w2, L0_ffn_b2):
    import jax
    import jax.numpy as jnp

    def _L0_tok_ref(x, w):
        import jax, jax.numpy as jnp
        import numpy as np
        VOCAB = 50257
        EMBED = 128
        return jnp.take(w, x, axis=0)

    def _L0_attn_ref(x, Wq, Wk, Wv, log_lambda):
        import jax, jax.numpy as jnp
        import numpy as np
        B, N, IN_F, OUT_F, HEAD_D = (4, 1024, 128, 128, 64)
        THRESHOLD_LAMBDA_MIN = 0.001
        Q = jnp.einsum('bni,di->bnd', x, Wq)
        K = jnp.einsum('bni,di->bnd', x, Wk)
        V = jnp.einsum('bni,oi->bno', x, Wv)
        q_sq = jnp.sum(Q * Q, axis=-1)
        k_sq = jnp.sum(K * K, axis=-1)
        cross = jnp.einsum('bnd,bmd->bnm', Q, K)
        dist_sq = jnp.maximum(q_sq[:, :, None] + k_sq[:, None, :] - 2.0 * cross, 0.0)
        lam = jnp.clip(jnp.exp(log_lambda[0]), THRESHOLD_LAMBDA_MIN, None)
        logits = -dist_sq / (2.0 * lam * lam)
        attn = jax.nn.softmax(logits, axis=-1)
        out = jnp.einsum('bnm,bmo->bno', attn, V)
        return out

    def _L0_ffn_ref(x, rw, rb, w1, b1, w2, b2):
        import jax, jax.numpy as jnp
        import numpy as np
        DIM, DEPTH, MULT = (128, 3, 4)
        E = 2 ** DEPTH
        HID = MULT * DIM
        B, S = (4, 256)

        def _leaf_probs(flat_x, rw, rb):
            n_tok = flat_x.shape[0]
            leaf = jnp.ones((n_tok, 1), dtype=flat_x.dtype)
            for d in range(DEPTH):
                off, n = (2 ** d - 1, 2 ** d)
                logits = flat_x @ rw[off:off + n].T + rb[off:off + n]
                p = jax.nn.sigmoid(logits)
                leaf = (leaf[:, :, None] * jnp.stack([1.0 - p, p], axis=2)).reshape(n_tok, 2 * n)
            return leaf
        b, s, dim = x.shape
        flat_x = x.reshape(b * s, dim)
        leaf_probs = _leaf_probs(flat_x, rw, rb)
        h = jnp.einsum('nd,edh->neh', flat_x, w1) + b1[None]
        h = jax.nn.gelu(h, approximate=False)
        y = jnp.einsum('neh,ehd->ned', h, w2) + b2[None]
        out = jnp.einsum('ned,ne->nd', y, leaf_probs)
        return out.reshape(b, s, dim)
    h = _L0_tok_ref(x, L0_tok_w)
    h = h + _L0_attn_ref(_layernorm(h, axis=-1), L0_attn_Wq, L0_attn_Wk, L0_attn_Wv, L0_attn_log_lambda)
    h = h + _L0_ffn_ref(_layernorm(h, axis=-1), L0_ffn_rw, L0_ffn_rb, L0_ffn_w1, L0_ffn_b1, L0_ffn_w2, L0_ffn_b2)
    return h

_drawn_inputs = setup_inputs


def setup_inputs(seed=0):
    import zlib

    import numpy as np

    out = dict(_drawn_inputs(seed))
    spreads = {}
    factors = {'L0_ffn_rb': 4.41, 'L0_ffn_b2': 3.03}
    for name, (base, spread) in spreads.items():
        noise = np.random.default_rng([zlib.crc32(name.encode()), seed]).standard_normal(out[name].shape)
        drawn = base * np.exp(spread * noise) if base else spread * noise
        out[name] = jnp.asarray(drawn.astype(out[name].dtype))
    for name, factor in factors.items():
        out[name] = (out[name] * factor).astype(out[name].dtype)
    return out
```

```python
import concourse.bass as bass
from concourse import mybir
from contextlib import ExitStack


def bass_lm_tower_kernel(
    nc: bass.Bass,
    x: bass.AP,
    tok_w: bass.AP,
    wq: bass.AP,
    wk: bass.AP,
    wv: bass.AP,
    log_lambda: bass.AP,
    rw: bass.AP,
    rb: bass.AP,
    w1: bass.AP,
    b1: bass.AP,
    w2: bass.AP,
    b2: bass.AP,
    out: bass.AP,
):
    f32 = mybir.dt.float32
    f32r = mybir.dt.float32r
    i32 = mybir.dt.int32
    ALU = mybir.AluOpType
    ACT = mybir.ActivationFunctionType
    AX = mybir.AxisListType

    P = 128
    NB, S = x.shape
    D = tok_w.shape[1]
    HD = wq.shape[0]
    E, _, HID = w1.shape
    NODES = rw.shape[0]
    GB = 4
    G = NB // GB
    N = GB * S
    KT = HID // P
    UT = 2
    UPE = KT // UT
    U = E * UPE
    HS = 4
    AUG = HD + 2
    LN_EPS = 1e-5
    LAM_MIN = 0.001
    ROWS = NODES + E + E * KT
    assert S == P and D == P and N * 4 == 2048 and UPE == 2

    b1_rows = b1.rearrange("e (k p) -> (e k) p", p=P)
    w2_d = w2.rearrange("e (k p) d -> e p k d", p=P)
    out_d = out.rearrange("b p d -> p b d")
    leaf_d = nc.dram_tensor("leaf_scratch", (G, E, N), f32, kind="Internal").ap()

    ctx = ExitStack()
    with ctx:
        def sb(name, shape, dt=f32):
            return ctx.enter_context(nc.sbuf_tensor(name, shape, dt))

        def sem(name):
            return ctx.enter_context(nc.semaphore(name))

        ident = sb("ident", [P, P])
        ids_rows = sb("ids_rows", [32, S], i32)
        ids_cols = sb("ids_cols", [P, 32], i32)
        h = sb("h", [P, NB, D])
        wqk_rows = sb("wqk_rows", [P, D])
        wv_rows = sb("wv_rows", [P, D])
        small_rows = sb("small_rows", [P, D])
        wqkv_t = sb("wqkv_t", [P, 2 * HD + D])
        small_t = sb("small_t", [P, ROWS])
        rb_bc = sb("rb_bc", [P, NODES])
        lam = sb("lam", [P, 6])
        neg_half = sb("neg_half", [P, GB])
        w1_raw = sb("w1_raw", [P, E, HID])
        w2_raw = sb("w2_raw", [P, E, KT, D])
        w1_hi = sb("w1_hi", [P, E, HID], f32r)
        w1_lo = sb("w1_lo", [P, E, HID], f32r)
        w2_hi = sb("w2_hi", [P, E, KT, D], f32r)
        w2_lo = sb("w2_lo", [P, E, KT, D], f32r)
        stats = sb("stats", [P, GB, 6])
        moment = sb("moment", [P, 5, GB])
        mean = sb("mean", [P, GB])
        veps = sb("veps", [P, GB])
        rstd = sb("rstd", [P, GB])
        xn = sb("xn", [P, GB, D])
        xn_t = sb("xn_t", [P, N])
        qk = sb("qk", [P, GB, 2, AUG])
        v = sb("v", [P, GB, D])
        sq = sb("sq", [P, GB, 2, HD])
        q_t = sb("q_t", [AUG, N])
        k_t = sb("k_t", [AUG, N])
        dist = sb("dist", [P, GB, S])
        dmin = sb("dmin", [P, GB])
        ebias = sb("ebias", [P, GB])
        prob = sb("prob", [P, GB, S])
        rowsum = sb("rowsum", [P, GB])
        rinv = sb("rinv", [P, GB])
        prob_t = sb("prob_t", [P, N])
        x_t = sb("x_t", [P, N])
        x_hi = sb("x_hi", [P, N], f32r)
        x_lo = sb("x_lo", [P, N], f32r)
        z = sb("z", [P, GB, NODES])
        th = sb("th", [P, GB, NODES])
        side = sb("side", [P, GB, NODES, 2])
        leaf2 = sb("leaf2", [P, GB, 2, 2])
        leaf3 = sb("leaf3", [P, GB, 4, 2])
        leaf_t = sb("leaf_t", [E, N])
        leaf_bc = sb("leaf_bc", [P, E, N])
        g_full = sb("g_full", [P, 2, UT * N])
        g_hi = sb("g_hi", [P, HS, UT * N], f32r)
        g_lo = sb("g_lo", [P, HS, UT * N], f32r)
        acc = sb("acc", [P, N])
        part = sb("part", [P, 2, N])

        hid = [ctx.enter_context(nc.psum_tensor(f"hid{i}", [P, UT * N], f32)) for i in range(2)]
        y = [ctx.enter_context(nc.psum_tensor(f"y{i}", [P, N], f32)) for i in range(2)]
        pa = [ctx.enter_context(nc.psum_tensor(f"pa{i}", [P, N], f32)) for i in range(2)]

        ids_cleared = sem("ids_cleared")
        ids_in = sem("ids_in")
        ids_turned = sem("ids_turned")
        rows_in = sem("rows_in")
        consts_in = sem("consts_in")
        weights_in = [sem(f"weights_in{e}") for e in range(E)]
        gathered_first = sem("gathered_first")
        gathered_rest = sem("gathered_rest")
        ident_zero = sem("ident_zero")
        ident_ready = sem("ident_ready")
        consts_set = sem("consts_set")
        rows_turned = sem("rows_turned")
        proj_ready = sem("proj_ready")
        small_ready = sem("small_ready")
        lam_exp = sem("lam_exp")
        lam_step = sem("lam_step")
        w_hi_done = sem("w_hi_done")
        w_lo_done = sem("w_lo_done")
        ln_stats = sem("ln_stats")
        ln_sums = sem("ln_sums")
        ln_moments = sem("ln_moments")
        ln_var = sem("ln_var")
        ln_rstd = sem("ln_rstd")
        ln_done = sem("ln_done")
        xn_turned = sem("xn_turned")
        xn_t_ready = sem("xn_t_ready")
        qkv_done = sem("qkv_done")
        qk_ready = sem("qk_ready")
        v_ready = sem("v_ready")
        sq_done = sem("sq_done")
        norms_done = sem("norms_done")
        qk_turned = sem("qk_turned")
        q_t_ready = sem("q_t_ready")
        k_t_ready = sem("k_t_ready")
        cross_done = sem("cross_done")
        dist_ready = sem("dist_ready")
        dmin_ready = sem("dmin_ready")
        ebias_ready = sem("ebias_ready")
        prob_ready = sem("prob_ready")
        rinv_ready = sem("rinv_ready")
        prob_turned = sem("prob_turned")
        prob_t_ready = sem("prob_t_ready")
        pv_done = sem("pv_done")
        h_ready = sem("h_ready")
        x_turned = sem("x_turned")
        x_t_ready = sem("x_t_ready")
        x_hi_ready = sem("x_hi_ready")
        x_lo_ready = sem("x_lo_ready")
        router_done = sem("router_done")
        z_ready = sem("z_ready")
        th_ready = sem("th_ready")
        side_ready = sem("side_ready")
        leaf2_ready = sem("leaf2_ready")
        leaf3_ready = sem("leaf3_ready")
        leaf_turned = sem("leaf_turned")
        leaf_t_ready = sem("leaf_t_ready")
        leaf_stored = sem("leaf_stored")
        leaf_first = sem("leaf_first")
        leaf_second = sem("leaf_second")
        up_done = sem("up_done")
        gelu_done = sem("gelu_done")
        g_hi_act = sem("g_hi_act")
        g_hi_dve = sem("g_hi_dve")
        g_lo_done = sem("g_lo_done")
        down_done = sem("down_done")
        mixed = sem("mixed")
        added = sem("added")
        acc_turned = sem("acc_turned")
        out_ready = sem("out_ready")
        out_stored = sem("out_stored")

        rw_t = small_t[:, 0:NODES]

        def b2_t(e):
            return small_t[:, NODES + e:NODES + e + 1]

        def b1_t(e, k):
            c = NODES + E + e * KT + k
            return small_t[:, c:c + 1]

        neg_s = lam[:, 4:5]
        pos_s = lam[:, 5:6]

        def rows(g):
            return h[:, bass.ds(g * GB, GB), :]

        def hi_on_act(u):
            return u % 2 == 0

        def wait_high(engine, g, u):
            alike = [w for w in range(U) if hi_on_act(w) == hi_on_act(u)]
            engine.wait_ge(g_hi_act if hi_on_act(u) else g_hi_dve, g * len(alike) + alike.index(u) + 1)

        block = ctx.enter_context(nc.Block())

        @block.sync
        def _(sp):
            sp.wait_ge(ids_cleared, 1)
            sp.dma_start(ids_rows[0:NB, :], x).then_inc(ids_in, 16)
            sp.dma_start(wqk_rows[0:HD, :], wq).then_inc(rows_in, 16)
            sp.dma_start(wqk_rows[HD:2 * HD, :], wk).then_inc(rows_in, 16)
            sp.dma_start(wv_rows[:, :], wv).then_inc(rows_in, 16)
            sp.dma_start(small_rows[0:NODES, :], rw).then_inc(rows_in, 16)
            sp.dma_start(small_rows[NODES:NODES + E, :], b2).then_inc(rows_in, 16)
            sp.dma_start(small_rows[NODES + E:ROWS, :], b1_rows).then_inc(rows_in, 16)
            for e in range(E):
                sp.dma_start(w1_raw[:, e, :], w1[e, :, :]).then_inc(weights_in[e], 16)
                sp.dma_start(w2_raw[:, e, :, :], w2_d[e, :, :, :]).then_inc(weights_in[e], 16)

            def spread_leaves(n, first):
                sp.wait_ge(leaf_t_ready, n + 1)
                sp.dma_start(leaf_d[bass.ds(n, 1), :, :].rearrange("a e t -> (a e) t"),
                             leaf_t[:, :]).then_inc(leaf_stored, 16)
                sp.wait_ge(leaf_stored, 16 * n + 16)
                for part_of, (done, e0) in enumerate(((leaf_first, 0), (leaf_second, E // 2))):
                    if not first:
                        sp.wait_ge(mixed, (n - 1) * E + e0 + E // 2)
                    src = leaf_d[bass.ds(n, 1), e0:e0 + E // 2, :].rearrange("a e t -> a (e t)")
                    sp.dma_start(leaf_bc[:, e0:e0 + E // 2, :].rearrange("p e t -> p (e t)"),
                                 src.to_broadcast([P, (E // 2) * N])).then_inc(done, 16)

            def store(g):
                sp.wait_ge(out_ready, g + 1)
                sp.dma_start(out_d[:, bass.ds(g * GB, GB), :], rows(g)).then_inc(out_stored, 16)

            spread_leaves(0, True)
            with sp.Fori(0, G - 1) as g:
                spread_leaves(g + 1, False)
                store(g)
            store(G - 1)
            sp.wait_ge(out_stored, 16 * G)

        @block.gpsimd
        def _(pool):
            nc.gpsimd.memset(ident[:, :], 0.0).then_inc(ident_zero, 1)
            nc.gpsimd.memset(neg_half[:, :], -0.5).then_inc(consts_set, 1)
            pool.wait_ge(ident_zero, 1)
            nc.gpsimd.affine_select(out=ident[:, :], in_=ident[:, :], compare_op=ALU.not_equal, fill=1.0,
                                    base=0, pattern=[[-1, P]], channel_multiplier=1).then_inc(ident_ready, 1)

            def gather(b, done):
                nc.gpsimd.indirect_dma_start(
                    out=h[:, b, :], out_offset=None, in_=tok_w,
                    in_offset=bass.IndirectOffsetOnAxis(ap=ids_cols[:, b:b + 1], axis=0)).then_inc(done, 16)

            def inverse_deviation(n, k):
                pool.wait_ge(ln_var, 2 * n + k + 1)
                nc.gpsimd.tensor_tensor(rstd[:, :], veps[:, :], neg_half[:, :], ALU.pow).then_inc(ln_rstd, 1)

            def weights_low(e):
                pool.wait_ge(w_hi_done, e + 1)
                nc.gpsimd.tensor_tensor(w1_lo[:, e, :], w1_raw[:, e, :], w1_hi[:, e, :].bitcast(f32), ALU.subtract)
                nc.gpsimd.tensor_tensor(w2_lo[:, e, :, :], w2_raw[:, e, :, :], w2_hi[:, e, :, :].bitcast(f32),
                                        ALU.subtract).then_inc(w_lo_done, 1)

            def add(g, e):
                pool.wait_ge(mixed, g * E + e + 1)
                if e > 1:
                    pool.wait_ge(added, g * (E - 1) + e - 1)
                nc.gpsimd.tensor_tensor(acc[:, :], acc[:, :], part[:, e % 2, :], ALU.add).then_inc(added, 1)

            pool.wait_ge(ids_turned, 1)
            pool.wait_ge(consts_set, 1)
            for b in range(GB):
                gather(b, gathered_first)
            inverse_deviation(0, 0)
            for e in range(3):
                weights_low(e)
            for b in range(GB, 2 * GB):
                gather(b, gathered_rest)
            inverse_deviation(0, 1)
            for e in range(3, E):
                weights_low(e)
                if e < 5:
                    for b in range(GB * (e - 1), GB * e):
                        gather(b, gathered_rest)

            def slots(g, n, ss, attention):
                for s in ss:
                    if s % 2 == 0 and s > 2:
                        add(g, s // 2 - 1)
                    if attention and s == 2:
                        inverse_deviation(n, 0)
                    if attention and s == 10:
                        inverse_deviation(n, 1)

            with pool.Fori(0, G - 1) as g:
                slots(g, g + 1, range(2, U), True)
                add(g, E - 1)
            slots(G - 1, G, range(2, U), False)
            add(G - 1, E - 1)

        @block.scalar
        def _(act):
            act.dma_start(rb_bc[:, :], rb.rearrange("(a n) -> a n", a=1).to_broadcast([P, NODES])).then_inc(consts_in, 16)
            act.dma_start(lam[:, 0:1], log_lambda.rearrange("(a n) -> a n", a=1).to_broadcast([P, 1])).then_inc(consts_in, 16)
            act.wait_ge(consts_in, 32)
            nc.scalar.activation(lam[:, 1:2], lam[:, 0:1], ACT.Exp).then_inc(lam_exp, 1)

            def turned(n):
                act.wait_ge(xn_turned, n + 1)
                nc.scalar.activation(xn_t[:, :], pa[0][:, :], ACT.Copy).then_inc(xn_t_ready, 1)

            def values(n):
                act.wait_ge(qkv_done, n + 1)
                nc.scalar.activation(v[:, :, :].rearrange("p b d -> p (b d)"), pa[1][:, :], ACT.Copy).then_inc(v_ready, 1)

            def queries(n):
                act.wait_ge(qk_turned, n + 1)
                nc.scalar.activation(q_t[:, :], pa[0][0:AUG, :], ACT.Copy).then_inc(q_t_ready, 1)

            def softmax(n):
                act.wait_ge(ebias_ready, n + 1)
                for b in range(GB):
                    last = nc.scalar.activation(prob[:, b, :], dist[:, b, :], ACT.Exp, bias=ebias[:, b:b + 1],
                                                scale=neg_s, accum_out=rowsum[:, b:b + 1])
                last.then_inc(prob_ready, 1)

            def probs_turned(n):
                act.wait_ge(prob_turned, n + 1)
                nc.scalar.activation(prob_t[:, :], pa[1][:, :], ACT.Copy).then_inc(prob_t_ready, 1)

            def expert_input(n):
                act.wait_ge(x_turned, n + 1)
                nc.scalar.activation(x_t[:, :], pa[1][:, :], ACT.Copy).then_inc(x_t_ready, 1)

            def input_high(n, first):
                act.wait_ge(x_t_ready, n + 1)
                if not first:
                    act.wait_ge(up_done, n * U * UT)
                nc.scalar.activation(x_hi[:, :], x_t[:, :], ACT.Copy).then_inc(x_hi_ready, 1)

            def router_tanh(n):
                act.wait_ge(z_ready, n + 1)
                nc.scalar.activation(th[:, :, :], z[:, :, :], ACT.Tanh, scale=0.5).then_inc(th_ready, 1)

            def leaves_turned(n):
                act.wait_ge(leaf_turned, n + 1)
                nc.scalar.activation(leaf_t[:, :], pa[0][0:E, :], ACT.Copy).then_inc(leaf_t_ready, 1)

            def gelu(g, u, first=False):
                e, kp = u // UPE, u % UPE
                for t in range(UT):
                    act.wait_ge(up_done, (g * U + u) * UT + t + 1)
                    if t == 0 and (not first or u >= 2):
                        act.wait_ge(g_lo_done, g * U + u - 1)
                    last = nc.scalar.activation(g_full[:, u % 2, t * N:(t + 1) * N],
                                                hid[u % 2][:, t * N:(t + 1) * N], ACT.Gelu,
                                                bias=b1_t(e, kp * UT + t))
                last.then_inc(gelu_done, 1)
                if hi_on_act(u):
                    act.wait_ge(gelu_done, g * U + u + 1)
                    if not first or u >= HS:
                        act.wait_ge(down_done, g * U + u - HS + 1)
                    nc.scalar.activation(g_hi[:, u % HS, :], g_full[:, u % 2, :], ACT.Copy).then_inc(g_hi_act, 1)

            turned(0)
            values(0)
            queries(0)
            act.wait_ge(lam_step, 3)
            softmax(0)
            probs_turned(0)
            for e in range(E):
                act.wait_ge(weights_in[e], 32)
                nc.scalar.activation(w1_hi[:, e, :], w1_raw[:, e, :], ACT.Copy)
                nc.scalar.activation(w2_hi[:, e, :, :], w2_raw[:, e, :, :], ACT.Copy).then_inc(w_hi_done, 1)
                if e == 2:
                    expert_input(0)
                    input_high(0, True)
            router_tanh(0)
            leaves_turned(0)
            gelu(0, 0, True)
            gelu(0, 1, True)

            def slots(g, n, ss, attention, first):
                for s in ss:
                    if attention and s == 13:
                        expert_input(n)
                        input_high(n, False)
                    if s + 2 < U:
                        gelu(g, s + 2, first)
                    elif attention:
                        gelu(n, s + 2 - U)
                    if attention:
                        if s == 3:
                            turned(n)
                        if s == 4:
                            values(n)
                        if s == 6:
                            queries(n)
                        if s == 8:
                            softmax(n)
                        if s == 9:
                            probs_turned(n)
                        if s == 14:
                            router_tanh(n)
                        if s == 15:
                            leaves_turned(n)
            slots(0, 1, range(0, 2), False, True)
            with act.Fori(0, G - 1) as g:
                slots(g, g + 1, range(2, U), True, False)
                slots(g + 1, g + 2, range(0, 2), False, False)
            slots(G - 1, G, range(2, U), False, False)

        @block.vector
        def _(dve):
            dve.memset(ids_rows[:, :], 0).then_inc(ids_cleared, 1)
            dve.memset(qk[:, :, 0, HD + 1:HD + 2], 1.0)
            dve.memset(qk[:, :, 1, HD:HD + 1], 1.0)
            dve.wait_ge(ids_in, 16)
            for j in range(S // 32):
                last = dve.transpose(ids_cols[32 * j:32 * j + 32, :], ids_rows[:, 32 * j:32 * j + 32])
            last.then_inc(ids_turned, 1)

            def layer_norm(n, k):
                for b in range(GB):
                    last = dve.bn_stats(stats[:, b, :], h[:, bass.ds(n * GB + b, 1), :].rearrange("p a d -> p (a d)"))
                last.then_inc(ln_stats, 1)
                dve.wait_ge(ln_stats, 2 * n + k + 1)
                dve.tensor_tensor(moment[:, 0, :], stats[:, :, 1], stats[:, :, 4], ALU.add)
                dve.tensor_tensor(moment[:, 1, :], stats[:, :, 1], stats[:, :, 4], ALU.subtract)
                dve.tensor_tensor(moment[:, 2, :], stats[:, :, 2], stats[:, :, 5], ALU.add).then_inc(ln_sums, 1)
                dve.wait_ge(ln_sums, 2 * n + k + 1)
                dve.tensor_scalar(mean[:, :], moment[:, 0, :], 0.5, None, ALU.mult)
                dve.scalar_tensor_tensor(out=moment[:, 3, :], in0=moment[:, 1, :], scalar=0.25, in1=moment[:, 1, :],
                                         op0=ALU.mult, op1=ALU.mult)
                dve.tensor_scalar(moment[:, 4, :], moment[:, 2, :], 1.0 / D, LN_EPS, ALU.mult,
                                  ALU.add).then_inc(ln_moments, 1)
                dve.wait_ge(ln_moments, 2 * n + k + 1)
                dve.tensor_tensor(veps[:, :], moment[:, 3, :], moment[:, 4, :], ALU.add).then_inc(ln_var, 1)

            def normalize(n, k):
                dve.wait_ge(ln_rstd, 2 * n + k + 1)
                for b in range(GB):
                    last = dve.tensor_scalar(xn[:, b, :], h[:, bass.ds(n * GB + b, 1), :].rearrange("p a d -> p (a d)"),
                                             mean[:, b:b + 1], rstd[:, b:b + 1], ALU.subtract, ALU.mult)
                last.then_inc(ln_done, 1)

            def queries_keys(n):
                dve.wait_ge(qkv_done, n + 1)
                dve.tensor_copy(qk[:, :, :, 0:HD],
                                pa[0][:, :].rearrange("p (b j c) -> p b j c", b=GB, j=2)).then_inc(qk_ready, 1)
                dve.wait_ge(qk_ready, n + 1)
                for j, scale in ((0, 1.0), (1, 0.25)):
                    last = dve.scalar_tensor_tensor(out=sq[:, :, j, :], in0=qk[:, :, j, 0:HD], scalar=scale,
                                                    in1=qk[:, :, j, 0:HD], op0=ALU.mult, op1=ALU.mult)
                last.then_inc(sq_done, 1)
                dve.wait_ge(sq_done, n + 1)
                for j in range(2):
                    last = dve.tensor_reduce(qk[:, :, j, HD + j:HD + j + 1], sq[:, :, j, :], AX.X, ALU.add)
                last.then_inc(norms_done, 1)

            def keys(n):
                dve.wait_ge(qk_turned, n + 1)
                dve.tensor_copy(k_t[:, :], pa[1][0:AUG, :]).then_inc(k_t_ready, 1)

            def distances(n):
                dve.wait_ge(cross_done, n + 1)
                dve.tensor_scalar(dist[:, :, :].rearrange("p b m -> p (b m)"), pa[0][:, :], 0.0, None,
                                  ALU.max).then_inc(dist_ready, 1)
                dve.wait_ge(dist_ready, n + 1)
                dve.tensor_reduce(dmin[:, :], dist[:, :, :], AX.X, ALU.min).then_inc(dmin_ready, 1)
                dve.wait_ge(dmin_ready, n + 1)
                dve.tensor_scalar(ebias[:, :], dmin[:, :], pos_s, None, ALU.mult).then_inc(ebias_ready, 1)

            def attend(n):
                dve.wait_ge(prob_ready, n + 1)
                dve.reciprocal(rinv[:, :], rowsum[:, :]).then_inc(rinv_ready, 1)
                dve.wait_ge(rinv_ready, n + 1)
                dve.wait_ge(pv_done, n + 1)
                for b in range(GB):
                    hb = h[:, bass.ds(n * GB + b, 1), :].rearrange("p a d -> p (a d)")
                    last = dve.scalar_tensor_tensor(out=hb, in0=pa[0][:, b * D:(b + 1) * D], scalar=rinv[:, b:b + 1],
                                                    in1=hb, op0=ALU.mult, op1=ALU.add)
                last.then_inc(h_ready, 1)
                dve.wait_ge(gathered_first, 16 * GB)
                dve.wait_ge(h_ready, n + 1)

            def input_low(n, first):
                dve.wait_ge(x_hi_ready, n + 1)
                dve.tensor_tensor(x_lo[:, :], x_t[:, :], x_hi[:, :].bitcast(f32), ALU.subtract).then_inc(x_lo_ready, 1)

            def router_bias(n):
                dve.wait_ge(router_done, n + 1)
                src = pa[0][:, 0:GB * 8].rearrange("p (b c) -> p b c", b=GB)[:, :, 0:NODES]
                dve.tensor_tensor(z[:, :, :], src, rb_bc[:, :].unsqueeze(1).to_broadcast([P, GB, NODES]),
                                  ALU.add).then_inc(z_ready, 1)

            def leaves(n):
                dve.wait_ge(th_ready, n + 1)
                dve.tensor_scalar(side[:, :, :, 0], th[:, :, :], -0.5, 0.5, ALU.mult, ALU.add)
                dve.tensor_scalar(side[:, :, :, 1], th[:, :, :], 0.5, 0.5, ALU.mult, ALU.add).then_inc(side_ready, 1)
                dve.wait_ge(side_ready, n + 1)
                dve.tensor_tensor(leaf2[:, :, :, :], side[:, :, 0, :].unsqueeze(3).to_broadcast([P, GB, 2, 2]),
                                  side[:, :, 1:3, :], ALU.mult).then_inc(leaf2_ready, 1)
                dve.wait_ge(leaf2_ready, n + 1)
                dve.tensor_tensor(leaf3[:, :, :, :],
                                  leaf2[:, :, :, :].rearrange("p b i j -> p b (i j)").unsqueeze(3).to_broadcast([P, GB, 4, 2]),
                                  side[:, :, 3:7, :], ALU.mult).then_inc(leaf3_ready, 1)

            def split(g, u, first=False):
                if not hi_on_act(u):
                    dve.wait_ge(gelu_done, g * U + u + 1)
                    if not first or u >= HS:
                        dve.wait_ge(down_done, g * U + u - HS + 1)
                    dve.tensor_copy(g_hi[:, u % HS, :], g_full[:, u % 2, :]).then_inc(g_hi_dve, 1)
                wait_high(dve, g, u)
                dve.tensor_tensor(g_lo[:, u % HS, :], g_full[:, u % 2, :], g_hi[:, u % HS, :].bitcast(f32),
                                  ALU.subtract).then_inc(g_lo_done, 1)

            def mix(g, e):
                dve.wait_ge(down_done, g * U + UPE * (e + 1))
                if e == 0:
                    dve.wait_ge(leaf_first, 16 * g + 16)
                if e == E // 2:
                    dve.wait_ge(leaf_second, 16 * g + 16)
                if e > 2:
                    dve.wait_ge(added, g * (E - 1) + e - 2)
                dst = acc[:, :] if e == 0 else part[:, e % 2, :]
                dve.scalar_tensor_tensor(out=dst, in0=y[e % 2][:, :], scalar=b2_t(e), in1=leaf_bc[:, e, :],
                                         op0=ALU.add, op1=ALU.mult).then_inc(mixed, 1)

            def finish(g):
                dve.wait_ge(acc_turned, g + 1)
                dve.tensor_tensor(rows(g), pa[1][:, :].rearrange("p (b d) -> p b d", b=GB), rows(g),
                                  ALU.add).then_inc(out_ready, 1)

            dve.wait_ge(rows_turned, 1)
            wt = pa[0][:, 0:2 * HD + D]
            dve.tensor_copy(wqkv_t[:, 0:HD], wt[:, 0:HD])
            dve.tensor_scalar(wqkv_t[:, HD:2 * HD], wt[:, HD:2 * HD], -2.0, None, ALU.mult)
            dve.tensor_copy(wqkv_t[:, 2 * HD:], wt[:, 2 * HD:]).then_inc(proj_ready, 1)
            dve.tensor_copy(small_t[:, :], pa[0][:, 2 * P:2 * P + ROWS]).then_inc(small_ready, 1)
            dve.wait_ge(lam_exp, 1)
            dve.tensor_scalar(lam[:, 2:3], lam[:, 1:2], LAM_MIN, 2.0 ** 0.5, ALU.max, ALU.mult).then_inc(lam_step, 1)
            dve.wait_ge(lam_step, 1)
            dve.tensor_tensor(lam[:, 3:4], lam[:, 2:3], lam[:, 2:3], ALU.mult).then_inc(lam_step, 1)
            dve.wait_ge(gathered_first, 16 * GB)
            layer_norm(0, 0)
            dve.wait_ge(lam_step, 2)
            dve.reciprocal(lam[:, 5:6], lam[:, 3:4]).then_inc(consts_set, 1)
            dve.wait_ge(consts_set, 2)
            dve.tensor_scalar(lam[:, 4:5], lam[:, 5:6], -1.0, None, ALU.mult).then_inc(lam_step, 1)
            normalize(0, 0)
            queries_keys(0)
            keys(0)
            distances(0)
            attend(0)
            layer_norm(0, 1)
            normalize(0, 1)
            input_low(0, True)
            router_bias(0)
            leaves(0)
            split(0, 0, True)
            split(0, 1, True)

            def slots(g, n, ss, attention, first):
                for s in ss:
                    if s % 2 == 0 and s > 0:
                        mix(g, s // 2 - 1)
                    if s == 0 and not first:
                        mix(g - 1, E - 1)
                    if attention:
                        if s == 2:
                            dve.wait_ge(gathered_rest, 16 * (NB - GB))
                            layer_norm(n, 0)
                            normalize(n, 0)
                        if s == 4:
                            queries_keys(n)
                        if s == 6:
                            keys(n)
                        if s == 7:
                            distances(n)
                        if s == 10:
                            attend(n)
                            layer_norm(n, 1)
                            normalize(n, 1)
                        if s == 13:
                            input_low(n, False)
                            router_bias(n)
                        if s == 14:
                            leaves(n)
                    if s == 1 and not first:
                        finish(g - 1)
                    if s + 2 < U:
                        split(g, s + 2, first)
                    elif attention:
                        split(n, s + 2 - U)

            slots(0, 1, range(0, 2), False, True)
            with dve.Fori(0, G - 1) as g:
                slots(g, g + 1, range(2, U), True, False)
                slots(g + 1, g + 2, range(0, 2), False, False)
            slots(G - 1, G, range(2, U), False, False)
            mix(G - 1, E - 1)
            finish(G - 1)

        @block.tensor
        def _(pe):
            mm, turn = nc.tensor.matmul, nc.tensor.transpose
            pe.wait_ge(ident_ready, 1)
            pe.wait_ge(rows_in, 16 * 6)
            turn(pa[0][:, 0:P], wqk_rows[:, :], ident[:, :])
            turn(pa[0][:, P:2 * P], wv_rows[:, :], ident[:, :])
            turn(pa[0][:, 2 * P:2 * P + ROWS], small_rows[0:ROWS, :], ident[0:ROWS, 0:ROWS]).then_inc(rows_turned, 1)

            def norm_turned(n, k):
                pe.wait_ge(ln_done, 2 * n + k + 1)
                dst = pa[k]
                for b in range(GB):
                    last = turn(dst[:, b * P:(b + 1) * P], xn[:, b, :], ident[:, :])
                last.then_inc((xn_turned, x_turned)[k], 1)

            def project(n):
                pe.wait_ge(xn_t_ready, n + 1)
                for b in range(GB):
                    tok = slice(b * P, (b + 1) * P)
                    mm(pa[0][:, tok], xn_t[:, tok], wqkv_t[:, 0:2 * HD], start=True, stop=True)
                    last = mm(pa[1][:, tok], xn_t[:, tok], wqkv_t[:, 2 * HD:], start=True, stop=True)
                last.then_inc(qkv_done, 1)

            def qk_turn(n):
                pe.wait_ge(v_ready, n + 1)
                pe.wait_ge(norms_done, n + 1)
                for j in range(2):
                    for b in range(GB):
                        last = turn(pa[j][0:AUG, b * P:(b + 1) * P], qk[:, b, j, :], ident[:, :])
                last.then_inc(qk_turned, 1)

            def distances(n):
                pe.wait_ge(q_t_ready, n + 1)
                pe.wait_ge(k_t_ready, n + 1)
                for b in range(GB):
                    last = mm(pa[0][:, b * P:(b + 1) * P], q_t[:, b * P:(b + 1) * P], k_t[:, b * P:(b + 1) * P],
                              start=True, stop=True)
                last.then_inc(cross_done, 1)

            def probs_turn(n):
                pe.wait_ge(prob_ready, n + 1)
                for b in range(GB):
                    last = turn(pa[1][:, b * P:(b + 1) * P], prob[:, b, :], ident[:, :])
                last.then_inc(prob_turned, 1)

            def attend(n):
                pe.wait_ge(prob_t_ready, n + 1)
                for b in range(GB):
                    last = mm(pa[0][:, b * D:(b + 1) * D], prob_t[:, b * P:(b + 1) * P], v[:, b, :], start=True, stop=True)
                last.then_inc(pv_done, 1)

            def router(n):
                pe.wait_ge(x_t_ready, n + 1)
                for b in range(GB):
                    last = mm(pa[0][:, 8 * b:8 * b + NODES], x_t[:, b * P:(b + 1) * P], rw_t, start=True, stop=True)
                last.then_inc(router_done, 1)

            def leaf_turn(n):
                pe.wait_ge(leaf3_ready, n + 1)
                for b in range(GB):
                    last = turn(pa[0][0:E, b * P:(b + 1) * P], leaf3[:, b, :, :].rearrange("p i j -> p (i j)"), ident[:, :])
                last.then_inc(leaf_turned, 1)

            def up(g, u, first=False):
                e, kp = u // UPE, u % UPE
                if kp == 0:
                    pe.wait_ge(w_hi_done, e + 1)
                    pe.wait_ge(w_lo_done, e + 1)
                if u == 0:
                    pe.wait_ge(x_hi_ready, g + 1)
                    pe.wait_ge(x_lo_ready, g + 1)
                if not first or u >= 2:
                    pe.wait_ge(gelu_done, g * U + u - 1)
                for t in range(UT):
                    k = kp * UT + t
                    dst = hid[u % 2][:, t * N:(t + 1) * N]
                    w_hi, w_lo = w1_hi[:, e, k * P:(k + 1) * P], w1_lo[:, e, k * P:(k + 1) * P]
                    mm(dst, w_hi, x_hi[:, :], start=True, stop=False)
                    mm(dst, w_lo, x_hi[:, :], start=False, stop=False)
                    mm(dst, w_hi, x_lo[:, :], start=False, stop=True).then_inc(up_done, 1)

            def down(g, u, first=False):
                e, kp = u // UPE, u % UPE
                dst = y[e % 2][:, :]
                wait_high(pe, g, u)
                if kp == 0 and e != 1 and (not first or e >= 2):
                    pe.wait_ge(mixed, g * E + e - 1)
                for t in range(UT):
                    k = kp * UT + t
                    mm(dst, w2_hi[:, e, k, :], g_hi[:, u % HS, t * N:(t + 1) * N], start=k == 0, stop=False)
                    mm(dst, w2_lo[:, e, k, :], g_hi[:, u % HS, t * N:(t + 1) * N], start=False, stop=False)
                pe.wait_ge(g_lo_done, g * U + u + 1)
                for t in range(UT):
                    k = kp * UT + t
                    last = mm(dst, w2_hi[:, e, k, :], g_lo[:, u % HS, t * N:(t + 1) * N], start=False, stop=k == KT - 1)
                last.then_inc(down_done, 1)

            def sum_turn(g):
                pe.wait_ge(added, (g + 1) * (E - 1))
                for b in range(GB):
                    last = turn(pa[1][:, b * P:(b + 1) * P], acc[:, b * P:(b + 1) * P], ident[:, :])
                last.then_inc(acc_turned, 1)

            pe.wait_ge(small_ready, 1)
            norm_turned(0, 0)
            pe.wait_ge(proj_ready, 1)
            project(0)
            qk_turn(0)
            distances(0)
            probs_turn(0)
            attend(0)
            norm_turned(0, 1)
            router(0)
            up(0, 0, True)
            leaf_turn(0)
            up(0, 1, True)

            def slots(g, n, ss, attention, first):
                for s in ss:
                    if s + 2 < U:
                        up(g, s + 2, first)
                    elif attention:
                        up(n, s + 2 - U)
                    if attention:
                        if s == 3:
                            norm_turned(n, 0)
                        if s == 4:
                            project(n)
                        if s == 6:
                            qk_turn(n)
                        if s == 7:
                            distances(n)
                        if s == 9:
                            probs_turn(n)
                        if s == 10:
                            attend(n)
                        if s == 12:
                            norm_turned(n, 1)
                        if s == 13:
                            router(n)
                        if s == 15:
                            leaf_turn(n)
                    if s == 1 and not first:
                        sum_turn(g - 1)
                    down(g, s, first)

            slots(0, 1, range(0, 2), False, True)
            with pe.Fori(0, G - 1) as g:
                slots(g, g + 1, range(2, U), True, False)
                slots(g + 1, g + 2, range(0, 2), False, False)
            slots(G - 1, G, range(2, U), False, False)
            sum_turn(G - 1)


_INS = ['x', 'L0_tok_w', 'L0_attn_Wq', 'L0_attn_Wk', 'L0_attn_Wv', 'L0_attn_log_lambda',
        'L0_ffn_rw', 'L0_ffn_rb', 'L0_ffn_w1', 'L0_ffn_b1', 'L0_ffn_w2', 'L0_ffn_b2']
_OUTS = [((16, 128, 128), 'float32')]


def kernel(**inputs):
    import numpy as _np
    import concourse.bacc as _bacc
    from concourse import mybir as _mybir
    from concourse.bass_utils import run_bass_kernel_spmd as _run

    nc = _bacc.Bacc("TRN2", target_bir_lowering=False, num_devices=1)
    arrays, args = {}, []
    for name in _INS:
        a = _np.ascontiguousarray(inputs[name])
        arrays[f"in_{name}_dram"] = a
        args.append(nc.dram_tensor(f"in_{name}_dram", a.shape, _mybir.dt.from_np(a.dtype), kind="ExternalInput").ap())
    for i, (shape, dtype) in enumerate(_OUTS):
        dt = _mybir.dt.from_np(_np.dtype(dtype))
        args.append(nc.dram_tensor(f"out_{i}_dram", shape, dt, kind="ExternalOutput").ap())
    bass_lm_tower_kernel(nc, *args)
    r = _run(nc, [arrays], core_ids=[0])
    got = tuple(r.results[0][f"out_{i}_dram"] for i in range(len(_OUTS)))
    return got[0]
```

```python
import concourse.bass as bass
from concourse import mybir
from collections import namedtuple
from contextlib import ExitStack


def bass_lm_tower_kernel(
    nc: bass.Bass,
    x: bass.AP,
    tok_w: bass.AP,
    wq: bass.AP,
    wk: bass.AP,
    wv: bass.AP,
    log_lambda: bass.AP,
    rw: bass.AP,
    rb: bass.AP,
    w1: bass.AP,
    b1: bass.AP,
    w2: bass.AP,
    b2: bass.AP,
    out: bass.AP,
):
    f32 = mybir.dt.float32
    f32r = mybir.dt.float32r
    i32 = mybir.dt.int32
    ALU = mybir.AluOpType
    ACT = mybir.ActivationFunctionType
    AX = mybir.AxisListType

    P = 128
    NB, S = x.shape
    D = tok_w.shape[1]
    HD = wq.shape[0]
    E, _, HID = w1.shape
    NODES = rw.shape[0]
    GB = 4
    G = NB // GB
    N = GB * S
    KT = HID // P
    UT = 2
    UPE = KT // UT
    U = E * UPE
    HS = 4
    AUG = HD + 2
    LN_EPS = 1e-5
    LAM_MIN = 0.001
    ROWS = NODES + E + E * KT
    assert S == P and D == P and N * 4 == 2048 and UPE == 2

    b1_rows = b1.rearrange("e (k p) -> (e k) p", p=P)
    w2_d = w2.rearrange("e (k p) d -> e p k d", p=P)
    out_d = out.rearrange("b p d -> p b d")
    leaf_d = nc.dram_tensor("leaf_scratch", (G, E, N), f32, kind="Internal").ap()

    ctx = ExitStack()
    with ctx:
        def sb(name, shape, dt=f32):
            return ctx.enter_context(nc.sbuf_tensor(name, shape, dt))

        def sem(name):
            return ctx.enter_context(nc.semaphore(name))

        ident = sb("ident", [P, P])
        ids_rows = sb("ids_rows", [32, S], i32)
        ids_cols = sb("ids_cols", [P, 32], i32)
        h = sb("h", [P, NB, D])
        wqk_rows = sb("wqk_rows", [P, D])
        wv_rows = sb("wv_rows", [P, D])
        small_rows = sb("small_rows", [P, D])
        wqkv_t = sb("wqkv_t", [P, 2 * HD + D])
        small_t = sb("small_t", [P, ROWS])
        rb_bc = sb("rb_bc", [P, NODES])
        lam = sb("lam", [P, 6])
        neg_half = sb("neg_half", [P, NB])
        w1_raw = sb("w1_raw", [P, E, HID])
        w2_raw = sb("w2_raw", [P, E, KT, D])
        w1_hi = sb("w1_hi", [P, E, HID], f32r)
        w1_lo = sb("w1_lo", [P, E, HID], f32r)
        w2_hi = sb("w2_hi", [P, E, KT, D], f32r)
        w2_lo = sb("w2_lo", [P, E, KT, D], f32r)
        stats = [sb("stats_attn", [P, NB, 6]), sb("stats_ffn", [P, GB, 6])]
        moment = sb("moment", [P, 5, NB])
        mean = [sb("mean_attn", [P, NB]), sb("mean_ffn", [P, GB])]
        veps = [sb("veps_attn", [P, NB]), sb("veps_ffn", [P, GB])]
        rstd = [sb("rstd_attn", [P, NB]), sb("rstd_ffn", [P, GB])]
        xn = sb("xn", [P, GB, D])
        xn_t = sb("xn_t", [P, N])
        qk = sb("qk", [P, GB, 2, AUG])
        v = sb("v", [P, GB, D])
        sq = sb("sq", [P, GB, 2, HD])
        q_t = sb("q_t", [AUG, N])
        k_t = sb("k_t", [AUG, N])
        dmin = sb("dmin", [P, GB])
        dclip = sb("dclip", [P, GB])
        dist = sb("dist", [P, GB, S])
        prob = sb("prob", [P, GB, S])
        rowsum = sb("rowsum", [P, GB])
        rinv = sb("rinv", [P, GB])
        prob_t = sb("prob_t", [P, N])
        x_t = sb("x_t", [P, N])
        x_hi = sb("x_hi", [P, N], f32r)
        x_lo = sb("x_lo", [P, N], f32r)
        z = sb("z", [P, GB, NODES])
        th = sb("th", [P, GB, NODES])
        side = sb("side", [P, GB, NODES, 2])
        leaf2 = sb("leaf2", [P, GB, 2, 2])
        leaf3 = sb("leaf3", [P, GB, 4, 2])
        leaf_t = sb("leaf_t", [E, N])
        leaf_bc = sb("leaf_bc", [P, E, N])
        g_full = sb("g_full", [P, 2, UT * N])
        g_hi = sb("g_hi", [P, HS, UT * N], f32r)
        g_lo = sb("g_lo", [P, HS, UT * N], f32r)
        acc = sb("acc", [P, N])
        part = sb("part", [P, 2, N])

        hid = [ctx.enter_context(nc.psum_tensor(f"hid{i}", [P, UT * N], f32)) for i in range(2)]
        y = [ctx.enter_context(nc.psum_tensor(f"y{i}", [P, N], f32)) for i in range(2)]
        pa = [ctx.enter_context(nc.psum_tensor(f"pa{i}", [P, N], f32)) for i in range(2)]

        ids_cleared = sem("ids_cleared")
        ids_in = sem("ids_in")
        ids_turned = sem("ids_turned")
        rows_in = sem("rows_in")
        consts_in = sem("consts_in")
        weights_in = [sem(f"weights_in{e}") for e in range(E)]
        gathered = [sem("gathered_half0"), sem("gathered_half1")]
        gathered_rest = sem("gathered_rest")
        ident_zero = sem("ident_zero")
        ident_ready = sem("ident_ready")
        consts_set = sem("consts_set")
        rows_turned = sem("rows_turned")
        proj_ready = sem("proj_ready")
        small_ready = sem("small_ready")
        lam_exp = sem("lam_exp")
        lam_step = sem("lam_step")
        w_hi_done = sem("w_hi_done")
        w_lo_done = sem("w_lo_done")
        ln_stats = [sem("ln_stats_attn"), sem("ln_stats_ffn")]
        ln_sums = [sem("ln_sums_attn"), sem("ln_sums_ffn")]
        ln_moments = [sem("ln_moments_attn"), sem("ln_moments_ffn")]
        ln_var = [sem("ln_var_attn"), sem("ln_var_ffn")]
        ln_rstd = [sem("ln_rstd_attn"), sem("ln_rstd_ffn")]
        ln_done = [sem("ln_done_attn"), sem("ln_done_ffn")]
        xn_turned = sem("xn_turned")
        xn_t_ready = sem("xn_t_ready")
        qkv_done = sem("qkv_done")
        qk_ready = sem("qk_ready")
        v_ready = sem("v_ready")
        sq_done = sem("sq_done")
        norms_done = sem("norms_done")
        qk_turned = sem("qk_turned")
        q_t_ready = sem("q_t_ready")
        k_t_ready = sem("k_t_ready")
        cross_done = sem("cross_done")
        dmin_ready = sem("dmin_ready")
        dclip_ready = sem("dclip_ready")
        dist_ready = sem("dist_ready")
        prob_ready = sem("prob_ready")
        rowsum_ready = sem("rowsum_ready")
        rinv_ready = sem("rinv_ready")
        prob_turned = sem("prob_turned")
        prob_t_ready = sem("prob_t_ready")
        pv_done = sem("pv_done")
        h_ready = sem("h_ready")
        x_turned = sem("x_turned")
        x_t_ready = sem("x_t_ready")
        x_hi_ready = sem("x_hi_ready")
        x_lo_ready = sem("x_lo_ready")
        router_done = sem("router_done")
        z_ready = sem("z_ready")
        th_ready = sem("th_ready")
        side_ready = sem("side_ready")
        leaf2_ready = sem("leaf2_ready")
        leaf3_ready = sem("leaf3_ready")
        leaf_turned = sem("leaf_turned")
        leaf_t_ready = sem("leaf_t_ready")
        leaf_stored = sem("leaf_stored")
        leaf_first = sem("leaf_first")
        leaf_second = sem("leaf_second")
        up_done = sem("up_done")
        gelu_done = sem("gelu_done")
        g_hi_act = sem("g_hi_act")
        g_hi_dve = sem("g_hi_dve")
        g_lo_done = sem("g_lo_done")
        down_done = sem("down_done")
        mixed = sem("mixed")
        added = sem("added")
        acc_turned = sem("acc_turned")
        out_ready = sem("out_ready")
        out_stored = sem("out_stored")

        rw_t = small_t[:, 0:NODES]

        def b2_t(e):
            return small_t[:, NODES + e:NODES + e + 1]

        def b1_t(e, k):
            c = NODES + E + e * KT + k
            return small_t[:, c:c + 1]

        neg_s = lam[:, 4:5]

        Chunk = namedtuple("Chunk", "group b0 nb banks turn")
        HALVES = [Chunk(0, i * GB // 2, GB // 2, bank, i + 1) for i, bank in enumerate((pa, y))]

        def whole(n):
            return Chunk(n, 0, GB, pa, n + len(HALVES))

        def last_turn(n):
            return n + len(HALVES)

        def tokens(c):
            return slice(c.b0 * S, (c.b0 + c.nb) * S)

        def batch_rows(c):
            return slice(c.b0, c.b0 + c.nb)

        def rows(g):
            return h[:, bass.ds(g * GB, GB), :]

        def hi_on_act(u):
            return u % 2 == 0

        def wait_high(engine, g, u):
            alike = [w for w in range(U) if hi_on_act(w) == hi_on_act(u)]
            engine.wait_ge(g_hi_act if hi_on_act(u) else g_hi_dve, g * len(alike) + alike.index(u) + 1)

        block = ctx.enter_context(nc.Block())

        @block.sync
        def _(sp):
            sp.wait_ge(ids_cleared, 1)
            sp.dma_start(ids_rows[0:NB, :], x).then_inc(ids_in, 16)
            sp.dma_start(wqk_rows[0:HD, :], wq).then_inc(rows_in, 16)
            sp.dma_start(wqk_rows[HD:2 * HD, :], wk).then_inc(rows_in, 16)
            sp.dma_start(wv_rows[:, :], wv).then_inc(rows_in, 16)
            sp.dma_start(small_rows[0:NODES, :], rw).then_inc(rows_in, 16)
            sp.dma_start(small_rows[NODES:NODES + E, :], b2).then_inc(rows_in, 16)
            sp.dma_start(small_rows[NODES + E:ROWS, :], b1_rows).then_inc(rows_in, 16)
            for i in range(2):
                sp.wait_ge(gathered[i], 16 * GB // 2)
            for e in range(E):
                sp.dma_start(w1_raw[:, e, :], w1[e, :, :]).then_inc(weights_in[e], 16)
                sp.dma_start(w2_raw[:, e, :, :], w2_d[e, :, :, :]).then_inc(weights_in[e], 16)

            def spread_leaves(n, first):
                sp.wait_ge(leaf_t_ready, n + 1)
                sp.dma_start(leaf_d[bass.ds(n, 1), :, :].rearrange("a e t -> (a e) t"),
                             leaf_t[:, :]).then_inc(leaf_stored, 16)
                sp.wait_ge(leaf_stored, 16 * n + 16)
                for part_of, (done, e0) in enumerate(((leaf_first, 0), (leaf_second, E // 2))):
                    if not first:
                        sp.wait_ge(mixed, (n - 1) * E + e0 + E // 2)
                    src = leaf_d[bass.ds(n, 1), e0:e0 + E // 2, :].rearrange("a e t -> a (e t)")
                    sp.dma_start(leaf_bc[:, e0:e0 + E // 2, :].rearrange("p e t -> p (e t)"),
                                 src.to_broadcast([P, (E // 2) * N])).then_inc(done, 16)

            def store(g):
                sp.wait_ge(out_ready, g + 1)
                sp.dma_start(out_d[:, bass.ds(g * GB, GB), :], rows(g)).then_inc(out_stored, 16)

            spread_leaves(0, True)
            with sp.Fori(0, G - 1) as g:
                spread_leaves(g + 1, False)
                store(g)
            store(G - 1)
            sp.wait_ge(out_stored, 16 * G)

        @block.gpsimd
        def _(pool):
            nc.gpsimd.memset(ident[:, :], 0.0).then_inc(ident_zero, 1)
            nc.gpsimd.memset(neg_half[:, :], -0.5).then_inc(consts_set, 1)
            pool.wait_ge(ident_zero, 1)
            nc.gpsimd.affine_select(out=ident[:, :], in_=ident[:, :], compare_op=ALU.not_equal, fill=1.0,
                                    base=0, pattern=[[-1, P]], channel_multiplier=1).then_inc(ident_ready, 1)

            def gather(b, done):
                nc.gpsimd.indirect_dma_start(
                    out=h[:, b, :], out_offset=None, in_=tok_w,
                    in_offset=bass.IndirectOffsetOnAxis(ap=ids_cols[:, b:b + 1], axis=0)).then_inc(done, 16)

            def inverse_deviation(k, turn, part):
                pool.wait_ge(ln_var[k], turn)
                nc.gpsimd.tensor_tensor(rstd[k][:, part], veps[k][:, part], neg_half[:, part],
                                        ALU.pow).then_inc(ln_rstd[k], 1)

            def weights_low(e):
                pool.wait_ge(w_hi_done, e + 1)
                nc.gpsimd.tensor_tensor(w1_lo[:, e, :], w1_raw[:, e, :], w1_hi[:, e, :].bitcast(f32), ALU.subtract)
                nc.gpsimd.tensor_tensor(w2_lo[:, e, :, :], w2_raw[:, e, :, :], w2_hi[:, e, :, :].bitcast(f32),
                                        ALU.subtract).then_inc(w_lo_done, 1)

            def add(g, e):
                pool.wait_ge(mixed, g * E + e + 1)
                if e > 1:
                    pool.wait_ge(added, g * (E - 1) + e - 1)
                nc.gpsimd.tensor_tensor(acc[:, :], acc[:, :], part[:, e % 2, :], ALU.add).then_inc(added, 1)

            pool.wait_ge(ids_turned, 1)
            pool.wait_ge(consts_set, 1)
            for c in HALVES:
                for b in range(c.b0, c.b0 + c.nb):
                    gather(b, gathered[c.turn - 1])
            for b in range(GB, 2 * GB):
                gather(b, gathered_rest)
            for c in HALVES:
                inverse_deviation(0, c.turn, batch_rows(c))
            for b in range(2 * GB, NB):
                gather(b, gathered_rest)
            weights_low(0)
            weights_low(1)
            inverse_deviation(0, len(HALVES) + 1, slice(GB, NB))
            for c in HALVES:
                inverse_deviation(1, c.turn, batch_rows(c))
            for e in range(2, E):
                weights_low(e)

            def slots(g, n, ss, attention):
                for s in ss:
                    if attention and s == 11:
                        inverse_deviation(1, last_turn(n), slice(0, GB))
                    if s % 2 == 0 and s > 2:
                        add(g, s // 2 - 1)

            with pool.Fori(0, G - 1) as g:
                slots(g, g + 1, range(2, U), True)
                add(g, E - 1)
            slots(G - 1, G, range(2, U), False)
            add(G - 1, E - 1)

        @block.scalar
        def _(act):
            act.dma_start(rb_bc[:, :], rb.rearrange("(a n) -> a n", a=1).to_broadcast([P, NODES])).then_inc(consts_in, 16)
            act.dma_start(lam[:, 0:1], log_lambda.rearrange("(a n) -> a n", a=1).to_broadcast([P, 1])).then_inc(consts_in, 16)
            act.wait_ge(consts_in, 32)
            nc.scalar.activation(lam[:, 1:2], lam[:, 0:1], ACT.Exp).then_inc(lam_exp, 1)

            def turned(c):
                act.wait_ge(xn_turned, c.turn)
                nc.scalar.activation(xn_t[:, tokens(c)], c.banks[0][:, 0:c.nb * S], ACT.Copy).then_inc(xn_t_ready, 1)

            def values(c):
                act.wait_ge(qkv_done, c.turn)
                nc.scalar.activation(v[:, batch_rows(c), :].rearrange("p b d -> p (b d)"), c.banks[1][:, 0:c.nb * D],
                                     ACT.Copy).then_inc(v_ready, 1)

            def queries(c):
                act.wait_ge(qk_turned, c.turn)
                nc.scalar.activation(q_t[:, tokens(c)], c.banks[0][0:AUG, 0:c.nb * S], ACT.Copy).then_inc(q_t_ready, 1)

            def softmax(c):
                act.wait_ge(dist_ready, c.turn)
                nc.scalar.activation(prob[:, batch_rows(c), :], dist[:, batch_rows(c), :], ACT.Exp,
                                     scale=neg_s).then_inc(prob_ready, 1)

            def expert_input(c):
                act.wait_ge(x_turned, c.turn)
                nc.scalar.activation(x_t[:, tokens(c)], c.banks[1][:, 0:c.nb * S], ACT.Copy).then_inc(x_t_ready, 1)

            def input_high(c, first=False):
                act.wait_ge(x_t_ready, c.turn)
                if not first:
                    act.wait_ge(up_done, c.group * U * UT)
                nc.scalar.activation(x_hi[:, tokens(c)], x_t[:, tokens(c)], ACT.Copy).then_inc(x_hi_ready, 1)

            def weights_high(e):
                act.wait_ge(weights_in[e], 32)
                nc.scalar.activation(w1_hi[:, e, :], w1_raw[:, e, :], ACT.Copy)
                nc.scalar.activation(w2_hi[:, e, :, :], w2_raw[:, e, :, :], ACT.Copy).then_inc(w_hi_done, 1)

            def router_tanh(n):
                act.wait_ge(z_ready, n + 1)
                nc.scalar.activation(th[:, :, :], z[:, :, :], ACT.Tanh, scale=0.5).then_inc(th_ready, 1)

            def leaves_turned(n):
                act.wait_ge(leaf_turned, n + 1)
                nc.scalar.activation(leaf_t[:, :], pa[0][0:E, :], ACT.Copy).then_inc(leaf_t_ready, 1)

            def gelu(g, u, first=False):
                e, kp = u // UPE, u % UPE
                for t in range(UT):
                    act.wait_ge(up_done, (g * U + u) * UT + t + 1)
                    if t == 0 and (not first or u >= 2):
                        act.wait_ge(g_lo_done, g * U + u - 1)
                    last = nc.scalar.activation(g_full[:, u % 2, t * N:(t + 1) * N],
                                                hid[u % 2][:, t * N:(t + 1) * N], ACT.Gelu,
                                                bias=b1_t(e, kp * UT + t))
                last.then_inc(gelu_done, 1)
                if hi_on_act(u):
                    act.wait_ge(gelu_done, g * U + u + 1)
                    if not first or u >= HS:
                        act.wait_ge(down_done, g * U + u - HS + 1)
                    nc.scalar.activation(g_hi[:, u % HS, :], g_full[:, u % 2, :], ACT.Copy).then_inc(g_hi_act, 1)

            weights_high(0)
            for stage, experts in ((turned, (1,)), (values, (2,)), (queries, (3,))):
                for c in HALVES:
                    stage(c)
                for e in experts:
                    weights_high(e)
            act.wait_ge(lam_step, 3)
            for c in HALVES:
                softmax(c)
            for e in (4, 5, 6):
                weights_high(e)
            for c in HALVES:
                expert_input(c)
                input_high(c, True)
            weights_high(7)
            router_tanh(0)
            leaves_turned(0)
            gelu(0, 0, True)
            gelu(0, 1, True)

            def slots(g, n, ss, attention, first):
                for s in ss:
                    c = whole(n) if attention else None
                    if attention and s == 3:
                        turned(c)
                    if attention and s == 6:
                        queries(c)
                    if attention and s == 13:
                        expert_input(c)
                        input_high(c)
                    if s + 2 < U:
                        gelu(g, s + 2, first)
                    elif attention:
                        gelu(n, s + 2 - U)
                    if attention and s == 3:
                        values(c)
                    if attention and s == 7:
                        softmax(c)
                    if attention and s == 14:
                        router_tanh(n)
                    if attention and s == 15:
                        leaves_turned(n)
            slots(0, 1, range(0, 2), False, True)
            with act.Fori(0, G - 1) as g:
                slots(g, g + 1, range(2, U), True, False)
                slots(g + 1, g + 2, range(0, 2), False, False)
            slots(G - 1, G, range(2, U), False, False)

        @block.vector
        def _(dve):
            dve.memset(ids_rows[:, :], 0).then_inc(ids_cleared, 1)
            dve.memset(qk[:, :, 0, HD + 1:HD + 2], 1.0)
            dve.memset(qk[:, :, 1, HD:HD + 1], 1.0)
            dve.wait_ge(ids_in, 16)
            for j in range(S // 32):
                last = dve.transpose(ids_cols[32 * j:32 * j + 32, :], ids_rows[:, 32 * j:32 * j + 32])
            last.then_inc(ids_turned, 1)

            def moments(k, turn, b0, nb, row):
                for b in range(b0, b0 + nb):
                    last = dve.bn_stats(stats[k][:, b, :], row(b))
                last.then_inc(ln_stats[k], 1)
                part = slice(b0, b0 + nb)
                dve.wait_ge(ln_stats[k], turn)
                dve.tensor_tensor(moment[:, 0, part], stats[k][:, part, 1], stats[k][:, part, 4], ALU.add)
                dve.tensor_tensor(moment[:, 1, part], stats[k][:, part, 1], stats[k][:, part, 4], ALU.subtract)
                dve.tensor_tensor(moment[:, 2, part], stats[k][:, part, 2], stats[k][:, part, 5],
                                  ALU.add).then_inc(ln_sums[k], 1)
                dve.wait_ge(ln_sums[k], turn)
                dve.tensor_scalar(mean[k][:, part], moment[:, 0, part], 0.5, None, ALU.mult)
                dve.scalar_tensor_tensor(out=moment[:, 3, part], in0=moment[:, 1, part], scalar=0.25,
                                         in1=moment[:, 1, part], op0=ALU.mult, op1=ALU.mult)
                dve.tensor_scalar(moment[:, 4, part], moment[:, 2, part], 1.0 / D, LN_EPS, ALU.mult,
                                  ALU.add).then_inc(ln_moments[k], 1)
                dve.wait_ge(ln_moments[k], turn)
                dve.tensor_tensor(veps[k][:, part], moment[:, 3, part], moment[:, 4, part], ALU.add).then_inc(ln_var[k], 1)

            def row_of(c, b):
                return h[:, bass.ds(c.group * GB + b, 1), :].rearrange("p a d -> p (a d)")

            def normalize(k, c):
                for b in range(c.b0, c.b0 + c.nb):
                    at = bass.ds(c.group * GB + b, 1) if k == 0 else slice(b, b + 1)
                    last = dve.tensor_scalar(xn[:, b, :], row_of(c, b), mean[k][:, at], rstd[k][:, at],
                                             ALU.subtract, ALU.mult)
                last.then_inc(ln_done[k], 1)

            def queries_keys(c):
                dve.wait_ge(qkv_done, c.turn)
                dve.tensor_copy(qk[:, batch_rows(c), :, 0:HD],
                                c.banks[0][:, 0:c.nb * 2 * HD].rearrange("p (b j c) -> p b j c", b=c.nb, j=2)).then_inc(qk_ready, 1)

            def norms(c):
                bs = batch_rows(c)
                dve.wait_ge(qk_ready, c.turn)
                for j, scale in ((0, 1.0), (1, 0.25)):
                    last = dve.scalar_tensor_tensor(out=sq[:, bs, j, :], in0=qk[:, bs, j, 0:HD], scalar=scale,
                                                    in1=qk[:, bs, j, 0:HD], op0=ALU.mult, op1=ALU.mult)
                last.then_inc(sq_done, 1)
                dve.wait_ge(sq_done, c.turn)
                for j in range(2):
                    last = dve.tensor_reduce(qk[:, bs, j, HD + j:HD + j + 1], sq[:, bs, j, :], AX.X, ALU.add)
                last.then_inc(norms_done, 1)

            def keys(c):
                dve.wait_ge(qk_turned, c.turn)
                dve.tensor_copy(k_t[:, tokens(c)], c.banks[1][0:AUG, 0:c.nb * S]).then_inc(k_t_ready, 1)

            def distances(c):
                bs = batch_rows(c)
                d = c.banks[0][:, 0:c.nb * S].rearrange("p (b m) -> p b m", b=c.nb)
                dve.wait_ge(cross_done, c.turn)
                dve.tensor_reduce(dmin[:, bs], d, AX.X, ALU.min).then_inc(dmin_ready, 1)
                dve.wait_ge(dmin_ready, c.turn)
                dve.tensor_scalar(dclip[:, bs], dmin[:, bs], 0.0, None, ALU.max).then_inc(dclip_ready, 1)
                dve.wait_ge(dclip_ready, c.turn)
                dve.scalar_tensor_tensor(out=dist[:, bs, :], in0=d, scalar=0.0,
                                         in1=dclip[:, bs].unsqueeze(2).to_broadcast([P, c.nb, S]),
                                         op0=ALU.max, op1=ALU.subtract).then_inc(dist_ready, 1)

            def row_sums(c):
                dve.wait_ge(prob_ready, c.turn)
                dve.tensor_reduce(rowsum[:, batch_rows(c)], prob[:, batch_rows(c), :], AX.X,
                                  ALU.add).then_inc(rowsum_ready, 1)

            def probs_turned(c):
                dve.wait_ge(prob_turned, c.turn)
                dve.tensor_copy(prob_t[:, tokens(c)], c.banks[1][:, 0:c.nb * S]).then_inc(prob_t_ready, 1)

            def attend(c):
                dve.wait_ge(rowsum_ready, c.turn)
                dve.reciprocal(rinv[:, batch_rows(c)], rowsum[:, batch_rows(c)]).then_inc(rinv_ready, 1)
                dve.wait_ge(rinv_ready, c.turn)
                dve.wait_ge(pv_done, c.turn)
                for i in range(c.nb):
                    b = c.b0 + i
                    last = dve.scalar_tensor_tensor(out=row_of(c, b), in0=c.banks[0][:, i * D:(i + 1) * D],
                                                    scalar=rinv[:, b:b + 1], in1=row_of(c, b), op0=ALU.mult, op1=ALU.add)
                last.then_inc(h_ready, 1)

            def expert_moments(c):
                dve.wait_ge(gathered[0], 16 * GB // 2)
                dve.wait_ge(h_ready, c.turn)
                moments(1, c.turn, c.b0, c.nb, lambda b: row_of(c, b))

            def expert_normalize(c):
                dve.wait_ge(ln_rstd[1], c.turn)
                normalize(1, c)

            def input_low(c):
                dve.wait_ge(x_hi_ready, c.turn)
                dve.tensor_tensor(x_lo[:, tokens(c)], x_t[:, tokens(c)], x_hi[:, tokens(c)].bitcast(f32),
                                  ALU.subtract).then_inc(x_lo_ready, 1)

            def router_bias(n):
                dve.wait_ge(router_done, n + 1)
                src = pa[0][:, 0:GB * 8].rearrange("p (b c) -> p b c", b=GB)[:, :, 0:NODES]
                dve.tensor_tensor(z[:, :, :], src, rb_bc[:, :].unsqueeze(1).to_broadcast([P, GB, NODES]),
                                  ALU.add).then_inc(z_ready, 1)

            def leaves(n):
                dve.wait_ge(th_ready, n + 1)
                dve.tensor_scalar(side[:, :, :, 0], th[:, :, :], -0.5, 0.5, ALU.mult, ALU.add)
                dve.tensor_scalar(side[:, :, :, 1], th[:, :, :], 0.5, 0.5, ALU.mult, ALU.add).then_inc(side_ready, 1)
                dve.wait_ge(side_ready, n + 1)
                dve.tensor_tensor(leaf2[:, :, :, :], side[:, :, 0, :].unsqueeze(3).to_broadcast([P, GB, 2, 2]),
                                  side[:, :, 1:3, :], ALU.mult).then_inc(leaf2_ready, 1)
                dve.wait_ge(leaf2_ready, n + 1)
                dve.tensor_tensor(leaf3[:, :, :, :],
                                  leaf2[:, :, :, :].rearrange("p b i j -> p b (i j)").unsqueeze(3).to_broadcast([P, GB, 4, 2]),
                                  side[:, :, 3:7, :], ALU.mult).then_inc(leaf3_ready, 1)

            def split(g, u, first=False):
                if not hi_on_act(u):
                    dve.wait_ge(gelu_done, g * U + u + 1)
                    if not first or u >= HS:
                        dve.wait_ge(down_done, g * U + u - HS + 1)
                    dve.tensor_copy(g_hi[:, u % HS, :], g_full[:, u % 2, :]).then_inc(g_hi_dve, 1)
                wait_high(dve, g, u)
                dve.tensor_tensor(g_lo[:, u % HS, :], g_full[:, u % 2, :], g_hi[:, u % HS, :].bitcast(f32),
                                  ALU.subtract).then_inc(g_lo_done, 1)

            def mix(g, e):
                dve.wait_ge(down_done, g * U + UPE * (e + 1))
                if e == 0:
                    dve.wait_ge(leaf_first, 16 * g + 16)
                if e == E // 2:
                    dve.wait_ge(leaf_second, 16 * g + 16)
                if e > 2:
                    dve.wait_ge(added, g * (E - 1) + e - 2)
                dst = acc[:, :] if e == 0 else part[:, e % 2, :]
                dve.scalar_tensor_tensor(out=dst, in0=y[e % 2][:, :], scalar=b2_t(e), in1=leaf_bc[:, e, :],
                                         op0=ALU.add, op1=ALU.mult).then_inc(mixed, 1)

            def finish(g):
                dve.wait_ge(acc_turned, g + 1)
                dve.tensor_tensor(rows(g), pa[1][:, :].rearrange("p (b d) -> p b d", b=GB), rows(g),
                                  ALU.add).then_inc(out_ready, 1)

            dve.wait_ge(rows_turned, 1)
            wt = pa[0][:, 0:2 * HD + D]
            dve.tensor_copy(wqkv_t[:, 0:HD], wt[:, 0:HD])
            dve.tensor_scalar(wqkv_t[:, HD:2 * HD], wt[:, HD:2 * HD], -2.0, None, ALU.mult)
            dve.tensor_copy(wqkv_t[:, 2 * HD:], wt[:, 2 * HD:]).then_inc(proj_ready, 1)
            dve.tensor_copy(small_t[:, :], pa[0][:, 2 * P:2 * P + ROWS]).then_inc(small_ready, 1)
            dve.wait_ge(lam_exp, 1)
            dve.tensor_scalar(lam[:, 2:3], lam[:, 1:2], LAM_MIN, 2.0 ** 0.5, ALU.max, ALU.mult).then_inc(lam_step, 1)
            dve.wait_ge(lam_step, 1)
            dve.tensor_tensor(lam[:, 3:4], lam[:, 2:3], lam[:, 2:3], ALU.mult).then_inc(lam_step, 1)
            dve.wait_ge(lam_step, 2)
            dve.reciprocal(lam[:, 5:6], lam[:, 3:4]).then_inc(consts_set, 1)
            dve.wait_ge(consts_set, 2)
            dve.tensor_scalar(lam[:, 4:5], lam[:, 5:6], -1.0, None, ALU.mult).then_inc(lam_step, 1)

            def attention_moments(c):
                dve.wait_ge(gathered[c.turn - 1], 16 * c.nb)
                moments(0, c.turn, c.b0, c.nb, lambda b: h[:, b, :])

            def attention_normalize(c):
                dve.wait_ge(ln_rstd[0], c.turn)
                normalize(0, c)

            for stage in (attention_moments, attention_normalize, queries_keys, norms, keys, distances):
                for c in HALVES:
                    stage(c)
            dve.wait_ge(gathered_rest, 16 * (NB - GB))
            moments(0, len(HALVES) + 1, GB, NB - GB, lambda b: h[:, b, :])
            for stage in (row_sums, probs_turned, attend, expert_moments, expert_normalize, input_low):
                for c in HALVES:
                    stage(c)
            router_bias(0)
            leaves(0)
            split(0, 0, True)
            split(0, 1, True)

            def slots(g, n, ss, attention, first):
                for s in ss:
                    if s % 2 == 0 and s > 0:
                        mix(g, s // 2 - 1)
                    if s == 0 and not first:
                        mix(g - 1, E - 1)
                    c = whole(n) if attention else None
                    if attention:
                        if s == 2:
                            dve.wait_ge(ln_rstd[0], len(HALVES) + 1)
                            normalize(0, c)
                        if s == 4:
                            queries_keys(c)
                        if s == 5:
                            norms(c)
                        if s == 6:
                            keys(c)
                        if s == 7:
                            distances(c)
                        if s == 8:
                            row_sums(c)
                            probs_turned(c)
                        if s == 10:
                            attend(c)
                        if s == 11:
                            expert_moments(c)
                        if s == 12:
                            expert_normalize(c)
                        if s == 13:
                            input_low(c)
                        if s == 14:
                            router_bias(n)
                        if s == 15:
                            leaves(n)
                    if s == 1 and not first:
                        finish(g - 1)
                    if s + 2 < U:
                        split(g, s + 2, first)
                    elif attention:
                        split(n, s + 2 - U)

            slots(0, 1, range(0, 2), False, True)
            with dve.Fori(0, G - 1) as g:
                slots(g, g + 1, range(2, U), True, False)
                slots(g + 1, g + 2, range(0, 2), False, False)
            slots(G - 1, G, range(2, U), False, False)
            mix(G - 1, E - 1)
            finish(G - 1)

        @block.tensor
        def _(pe):
            mm, turn = nc.tensor.matmul, nc.tensor.transpose
            pe.wait_ge(ident_ready, 1)
            pe.wait_ge(rows_in, 16 * 6)
            turn(pa[0][:, 0:P], wqk_rows[:, :], ident[:, :])
            turn(pa[0][:, P:2 * P], wv_rows[:, :], ident[:, :])
            turn(pa[0][:, 2 * P:2 * P + ROWS], small_rows[0:ROWS, :], ident[0:ROWS, 0:ROWS]).then_inc(rows_turned, 1)

            def norm_turn(k, c):
                pe.wait_ge(ln_done[k], c.turn)
                for i in range(c.nb):
                    last = turn(c.banks[k][:, i * P:(i + 1) * P], xn[:, c.b0 + i, :], ident[:, :])
                last.then_inc((xn_turned, x_turned)[k], 1)

            def project(c):
                pe.wait_ge(xn_t_ready, c.turn)
                for i in range(c.nb):
                    x_b, at = xn_t[:, (c.b0 + i) * P:(c.b0 + i + 1) * P], slice(i * P, (i + 1) * P)
                    mm(c.banks[0][:, at], x_b, wqkv_t[:, 0:2 * HD], start=True, stop=True)
                    last = mm(c.banks[1][:, at], x_b, wqkv_t[:, 2 * HD:], start=True, stop=True)
                last.then_inc(qkv_done, 1)

            def qk_turn(c):
                pe.wait_ge(v_ready, c.turn)
                pe.wait_ge(norms_done, c.turn)
                for j in range(2):
                    for i in range(c.nb):
                        last = turn(c.banks[j][0:AUG, i * P:(i + 1) * P], qk[:, c.b0 + i, j, :], ident[:, :])
                last.then_inc(qk_turned, 1)

            def distances(c):
                pe.wait_ge(q_t_ready, c.turn)
                pe.wait_ge(k_t_ready, c.turn)
                for i in range(c.nb):
                    tok = slice((c.b0 + i) * P, (c.b0 + i + 1) * P)
                    last = mm(c.banks[0][:, i * P:(i + 1) * P], q_t[:, tok], k_t[:, tok], start=True, stop=True)
                last.then_inc(cross_done, 1)

            def probs_turn(c):
                pe.wait_ge(prob_ready, c.turn)
                for i in range(c.nb):
                    last = turn(c.banks[1][:, i * P:(i + 1) * P], prob[:, c.b0 + i, :], ident[:, :])
                last.then_inc(prob_turned, 1)

            def attend(c):
                pe.wait_ge(prob_t_ready, c.turn)
                for i in range(c.nb):
                    b = c.b0 + i
                    last = mm(c.banks[0][:, i * D:(i + 1) * D], prob_t[:, b * P:(b + 1) * P], v[:, b, :],
                              start=True, stop=True)
                last.then_inc(pv_done, 1)

            def router(n):
                pe.wait_ge(x_t_ready, last_turn(n))
                for b in range(GB):
                    last = mm(pa[0][:, 8 * b:8 * b + NODES], x_t[:, b * P:(b + 1) * P], rw_t, start=True, stop=True)
                last.then_inc(router_done, 1)

            def leaf_turn(n):
                pe.wait_ge(leaf3_ready, n + 1)
                for b in range(GB):
                    last = turn(pa[0][0:E, b * P:(b + 1) * P], leaf3[:, b, :, :].rearrange("p i j -> p (i j)"), ident[:, :])
                last.then_inc(leaf_turned, 1)

            def up(g, u, first=False):
                e, kp = u // UPE, u % UPE
                if kp == 0:
                    pe.wait_ge(w_hi_done, e + 1)
                    pe.wait_ge(w_lo_done, e + 1)
                if u == 0:
                    pe.wait_ge(x_hi_ready, last_turn(g))
                    pe.wait_ge(x_lo_ready, last_turn(g))
                if not first or u >= 2:
                    pe.wait_ge(gelu_done, g * U + u - 1)
                for t in range(UT):
                    k = kp * UT + t
                    dst = hid[u % 2][:, t * N:(t + 1) * N]
                    w_hi, w_lo = w1_hi[:, e, k * P:(k + 1) * P], w1_lo[:, e, k * P:(k + 1) * P]
                    mm(dst, w_hi, x_hi[:, :], start=True, stop=False)
                    mm(dst, w_lo, x_hi[:, :], start=False, stop=False)
                    mm(dst, w_hi, x_lo[:, :], start=False, stop=True).then_inc(up_done, 1)

            def down(g, u, first=False):
                e, kp = u // UPE, u % UPE
                dst = y[e % 2][:, :]
                wait_high(pe, g, u)
                if kp == 0 and e != 1 and (not first or e >= 2):
                    pe.wait_ge(mixed, g * E + e - 1)
                for t in range(UT):
                    k = kp * UT + t
                    mm(dst, w2_hi[:, e, k, :], g_hi[:, u % HS, t * N:(t + 1) * N], start=k == 0, stop=False)
                    mm(dst, w2_lo[:, e, k, :], g_hi[:, u % HS, t * N:(t + 1) * N], start=False, stop=False)
                pe.wait_ge(g_lo_done, g * U + u + 1)
                for t in range(UT):
                    k = kp * UT + t
                    last = mm(dst, w2_hi[:, e, k, :], g_lo[:, u % HS, t * N:(t + 1) * N], start=False, stop=k == KT - 1)
                last.then_inc(down_done, 1)

            def sum_turn(g):
                pe.wait_ge(added, (g + 1) * (E - 1))
                for b in range(GB):
                    last = turn(pa[1][:, b * P:(b + 1) * P], acc[:, b * P:(b + 1) * P], ident[:, :])
                last.then_inc(acc_turned, 1)

            pe.wait_ge(small_ready, 1)
            for c in HALVES:
                norm_turn(0, c)
            pe.wait_ge(proj_ready, 1)
            for stage in (project, qk_turn, distances, probs_turn, attend):
                for c in HALVES:
                    stage(c)
            for c in HALVES:
                norm_turn(1, c)
            router(0)
            up(0, 0, True)
            leaf_turn(0)
            up(0, 1, True)

            def slots(g, n, ss, attention, first):
                for s in ss:
                    if s + 2 < U:
                        up(g, s + 2, first)
                    elif attention:
                        up(n, s + 2 - U)
                    c = whole(n) if attention else None
                    if attention:
                        if s == 3:
                            project(c)
                        if s == 9:
                            attend(c)
                        if s == 14:
                            router(n)
                        if s == 15:
                            leaf_turn(n)
                    if s == 1 and not first:
                        sum_turn(g - 1)
                    down(g, s, first)
                    if attention:
                        if s == 2:
                            norm_turn(0, c)
                        if s == 5:
                            qk_turn(c)
                        if s == 6:
                            distances(c)
                        if s == 8:
                            probs_turn(c)
                        if s == 12:
                            norm_turn(1, c)

            slots(0, 1, range(0, 2), False, True)
            with pe.Fori(0, G - 1) as g:
                slots(g, g + 1, range(2, U), True, False)
                slots(g + 1, g + 2, range(0, 2), False, False)
            slots(G - 1, G, range(2, U), False, False)
            sum_turn(G - 1)


_INS = ['x', 'L0_tok_w', 'L0_attn_Wq', 'L0_attn_Wk', 'L0_attn_Wv', 'L0_attn_log_lambda',
        'L0_ffn_rw', 'L0_ffn_rb', 'L0_ffn_w1', 'L0_ffn_b1', 'L0_ffn_w2', 'L0_ffn_b2']
_OUTS = [((16, 128, 128), 'float32')]


def kernel(**inputs):
    import numpy as _np
    import concourse.bacc as _bacc
    from concourse import mybir as _mybir
    from concourse.bass_utils import run_bass_kernel_spmd as _run

    nc = _bacc.Bacc("TRN2", target_bir_lowering=False, num_devices=1)
    arrays, args = {}, []
    for name in _INS:
        a = _np.ascontiguousarray(inputs[name])
        arrays[f"in_{name}_dram"] = a
        args.append(nc.dram_tensor(f"in_{name}_dram", a.shape, _mybir.dt.from_np(a.dtype), kind="ExternalInput").ap())
    for i, (shape, dtype) in enumerate(_OUTS):
        dt = _mybir.dt.from_np(_np.dtype(dtype))
        args.append(nc.dram_tensor(f"out_{i}_dram", shape, dt, kind="ExternalOutput").ap())
    bass_lm_tower_kernel(nc, *args)
    r = _run(nc, [arrays], core_ids=[0])
    got = tuple(r.results[0][f"out_{i}_dram"] for i in range(len(_OUTS)))
    return got[0]
```

```python
import concourse.bass as bass
from concourse import mybir
from collections import namedtuple
from contextlib import ExitStack


def bass_lm_tower_kernel(
    nc: bass.Bass,
    x: bass.AP,
    tok_w: bass.AP,
    wq: bass.AP,
    wk: bass.AP,
    wv: bass.AP,
    log_lambda: bass.AP,
    rw: bass.AP,
    rb: bass.AP,
    w1: bass.AP,
    b1: bass.AP,
    w2: bass.AP,
    b2: bass.AP,
    out: bass.AP,
):
    f32 = mybir.dt.float32
    f32r = mybir.dt.float32r
    i32 = mybir.dt.int32
    ALU = mybir.AluOpType
    ACT = mybir.ActivationFunctionType
    AX = mybir.AxisListType

    P = 128
    NB, S = x.shape
    D = tok_w.shape[1]
    HD = wq.shape[0]
    E, _, HID = w1.shape
    NODES = rw.shape[0]
    GB = 4
    G = NB // GB
    N = GB * S
    KT = HID // P
    UT = 2
    UPE = KT // UT
    U = E * UPE
    HS = 4
    AUG = HD + 2
    LN_EPS = 1e-5
    LAM_MIN = 0.001
    ROWS = NODES + E + E * KT
    assert S == P and D == P and N * 4 == 2048 and UPE == 2

    b1_rows = b1.rearrange("e (k p) -> (e k) p", p=P)
    w2_d = w2.rearrange("e (k p) d -> e p k d", p=P)
    out_d = out.rearrange("b p d -> p b d")
    leaf_d = nc.dram_tensor("leaf_scratch", (G, E, N), f32, kind="Internal").ap()

    ctx = ExitStack()
    with ctx:
        def sb(name, shape, dt=f32):
            return ctx.enter_context(nc.sbuf_tensor(name, shape, dt))

        def sem(name):
            return ctx.enter_context(nc.semaphore(name))

        ident = sb("ident", [P, P])
        ids_rows = sb("ids_rows", [32, S], i32)
        ids_cols = sb("ids_cols", [P, 32], i32)
        h = sb("h", [P, NB, D])
        wqk_rows = sb("wqk_rows", [P, D])
        wv_rows = sb("wv_rows", [P, D])
        small_rows = sb("small_rows", [P, D])
        wqkv_t = sb("wqkv_t", [P, 2 * HD + D])
        small_t = sb("small_t", [P, ROWS])
        rb_bc = sb("rb_bc", [P, NODES])
        lam = sb("lam", [P, 6])
        warm = sb("warm", [P, 1])
        neg_half = sb("neg_half", [P, NB])
        w1_raw = sb("w1_raw", [P, E, HID])
        w2_raw = sb("w2_raw", [P, E, KT, D])
        w1_hi = sb("w1_hi", [P, E, HID], f32r)
        w1_lo = sb("w1_lo", [P, E, HID], f32r)
        w2_hi = sb("w2_hi", [P, E, KT, D], f32r)
        w2_lo = sb("w2_lo", [P, E, KT, D], f32r)
        stats = [sb("stats_attn", [P, NB, 6]), sb("stats_ffn", [P, GB, 6])]
        moment = [sb("moment_attn", [P, NB, 2]), sb("moment_ffn", [P, GB, 2])]
        veps = [sb("veps_attn", [P, NB]), sb("veps_ffn", [P, GB])]
        rstd = [sb("rstd_attn", [P, NB]), sb("rstd_ffn", [P, GB])]
        xn = sb("xn", [P, GB, D])
        xn_t = sb("xn_t", [P, N])
        qk = sb("qk", [P, GB, 2, AUG])
        v = sb("v", [P, GB, D + 1])
        sq = sb("sq", [P, GB, 2, HD])
        q_t = sb("q_t", [AUG, N])
        k_t = sb("k_t", [AUG, N])
        dmin = sb("dmin", [P, GB])
        dclip = sb("dclip", [P, GB])
        dist = sb("dist", [P, GB, S])
        prob = sb("prob", [P, GB, S])
        rinv = sb("rinv", [P, GB])
        prob_t = sb("prob_t", [P, N])
        x_t = sb("x_t", [P, N])
        x_hi = sb("x_hi", [P, N], f32r)
        x_lo = sb("x_lo", [P, N], f32r)
        z = sb("z", [P, GB, NODES])
        th = sb("th", [P, GB, NODES])
        side = sb("side", [P, GB, NODES, 2])
        leaf2 = sb("leaf2", [P, GB, 2, 2])
        leaf3 = sb("leaf3", [P, GB, 4, 2])
        leaf_t = sb("leaf_t", [E, N])
        leaf_bc = sb("leaf_bc", [P, E, N])
        g_full = sb("g_full", [P, 2, UT * N])
        g_hi = sb("g_hi", [P, HS, UT * N], f32r)
        g_lo = sb("g_lo", [P, HS, UT * N], f32r)
        acc = sb("acc", [P, N])
        part = sb("part", [P, 2, N])

        hid = [ctx.enter_context(nc.psum_tensor(f"hid{i}", [P, UT * N], f32)) for i in range(2)]
        y = [ctx.enter_context(nc.psum_tensor(f"y{i}", [P, N], f32)) for i in range(2)]
        pa = [ctx.enter_context(nc.psum_tensor(f"pa{i}", [P, N], f32)) for i in range(2)]

        ids_cleared = sem("ids_cleared")
        ids_in = sem("ids_in")
        ids_turned = sem("ids_turned")
        rows_in = sem("rows_in")
        lambda_in = sem("lambda_in")
        bias_in = sem("bias_in")
        weights_in = [sem(f"weights_in{e}") for e in range(E)]
        gathered = [sem("gathered_half0"), sem("gathered_half1")]
        gathered_rest = sem("gathered_rest")
        ident_zero = sem("ident_zero")
        ident_ready = sem("ident_ready")
        neg_half_set = sem("neg_half_set")
        rows_turned = sem("rows_turned")
        proj_ready = sem("proj_ready")
        small_ready = sem("small_ready")
        lam_exp = sem("lam_exp")
        lam_step = sem("lam_step")
        w_hi_done = sem("w_hi_done")
        w_lo_done = sem("w_lo_done")
        ln_stats = [sem("ln_stats_attn"), sem("ln_stats_ffn")]
        ln_moments = [sem("ln_moments_attn"), sem("ln_moments_ffn")]
        ln_var = [sem("ln_var_attn"), sem("ln_var_ffn")]
        ln_rstd = [sem("ln_rstd_attn"), sem("ln_rstd_ffn")]
        ln_done = [sem("ln_done_attn"), sem("ln_done_ffn")]
        xn_turned = sem("xn_turned")
        xn_t_ready = sem("xn_t_ready")
        qk_done = sem("qk_done")
        v_done = sem("v_done")
        qk_ready = sem("qk_ready")
        v_ready = sem("v_ready")
        sq_done = sem("sq_done")
        norms_done = sem("norms_done")
        qk_turned = sem("qk_turned")
        q_t_ready = sem("q_t_ready")
        k_t_ready = sem("k_t_ready")
        cross_done = sem("cross_done")
        dmin_ready = sem("dmin_ready")
        dclip_ready = sem("dclip_ready")
        dist_ready = sem("dist_ready")
        prob_ready = sem("prob_ready")
        rinv_ready = sem("rinv_ready")
        prob_turned = sem("prob_turned")
        prob_t_ready = sem("prob_t_ready")
        pv_done = sem("pv_done")
        h_ready = sem("h_ready")
        x_turned = sem("x_turned")
        x_t_ready = sem("x_t_ready")
        x_hi_ready = sem("x_hi_ready")
        x_lo_ready = sem("x_lo_ready")
        router_done = sem("router_done")
        z_ready = sem("z_ready")
        th_ready = sem("th_ready")
        side_ready = sem("side_ready")
        leaf2_ready = sem("leaf2_ready")
        leaf3_ready = sem("leaf3_ready")
        leaf_turned = sem("leaf_turned")
        leaf_t_ready = sem("leaf_t_ready")
        leaf_stored = sem("leaf_stored")
        leaf_first = sem("leaf_first")
        leaf_second = sem("leaf_second")
        up_done = sem("up_done")
        gelu_done = sem("gelu_done")
        g_hi_act = sem("g_hi_act")
        g_hi_dve = sem("g_hi_dve")
        g_lo_done = sem("g_lo_done")
        down_done = sem("down_done")
        mixed = sem("mixed")
        added = sem("added")
        acc_turned = sem("acc_turned")
        out_ready = sem("out_ready")
        out_stored = sem("out_stored")
        tail_mixed = sem("tail_mixed")
        tail_added = sem("tail_added")
        tail_turned = sem("tail_turned")
        tail_ready = sem("tail_ready")

        rw_t = small_t[:, 0:NODES]

        def b2_t(e):
            return small_t[:, NODES + e:NODES + e + 1]

        def b1_t(e, k):
            c = NODES + E + e * KT + k
            return small_t[:, c:c + 1]

        neg_s = lam[:, 4:5]

        Chunk = namedtuple("Chunk", "group b0 nb banks turn")
        HALVES = [Chunk(0, i * GB // 2, GB // 2, bank, i + 1) for i, bank in enumerate((pa, y))]

        def whole(n):
            return Chunk(n, 0, GB, pa, n + len(HALVES))

        def last_turn(n):
            return n + len(HALVES)

        def tokens(c):
            return slice(c.b0 * S, (c.b0 + c.nb) * S)

        def attended(c, i):
            per_bank = c.nb // 2
            at = i % per_bank * (D + 1)
            return c.banks[i // per_bank][:, at:at + D + 1]

        def batch_rows(c):
            return slice(c.b0, c.b0 + c.nb)

        def rows(g):
            return h[:, bass.ds(g * GB, GB), :]

        def hi_on_act(u):
            return u not in (1, 6, 9, 10, 15)

        def wait_high(engine, g, u):
            alike = [w for w in range(U) if hi_on_act(w) == hi_on_act(u)]
            engine.wait_ge(g_hi_act if hi_on_act(u) else g_hi_dve, g * len(alike) + alike.index(u) + 1)

        block = ctx.enter_context(nc.Block())

        @block.sync
        def _(sp):
            sp.wait_ge(ids_cleared, 1)
            sp.dma_start(ids_rows[0:NB, :], x).then_inc(ids_in, 16)
            sp.dma_start(wqk_rows[0:HD, :], wq).then_inc(rows_in, 16)
            sp.dma_start(wqk_rows[HD:2 * HD, :], wk).then_inc(rows_in, 16)
            sp.dma_start(wv_rows[:, :], wv).then_inc(rows_in, 16)
            sp.dma_start(small_rows[0:NODES, :], rw).then_inc(rows_in, 16)
            sp.dma_start(small_rows[NODES:NODES + E, :], b2).then_inc(rows_in, 16)
            sp.dma_start(small_rows[NODES + E:ROWS, :], b1_rows).then_inc(rows_in, 16)
            sp.dma_start(rb_bc[:, :], rb.rearrange("(a n) -> a n", a=1).to_broadcast([P, NODES])).then_inc(bias_in, 16)
            for i in range(2):
                sp.wait_ge(gathered[i], 16 * GB // 2)
            for e in range(E):
                sp.dma_start(w1_raw[:, e, :], w1[e, :, :]).then_inc(weights_in[e], 16)
                sp.dma_start(w2_raw[:, e, :, :], w2_d[e, :, :, :]).then_inc(weights_in[e], 16)

            def spread_leaves(n, first):
                sp.wait_ge(leaf_t_ready, n + 1)
                sp.dma_start(leaf_d[bass.ds(n, 1), :, :].rearrange("a e t -> (a e) t"),
                             leaf_t[:, :]).then_inc(leaf_stored, 16)
                sp.wait_ge(leaf_stored, 16 * n + 16)
                for part_of, (done, e0) in enumerate(((leaf_first, 0), (leaf_second, E // 2))):
                    if not first:
                        sp.wait_ge(mixed, (n - 1) * E + e0 + E // 2)
                    src = leaf_d[bass.ds(n, 1), e0:e0 + E // 2, :].rearrange("a e t -> a (e t)")
                    sp.dma_start(leaf_bc[:, e0:e0 + E // 2, :].rearrange("p e t -> p (e t)"),
                                 src.to_broadcast([P, (E // 2) * N])).then_inc(done, 16)

            def store(g):
                sp.wait_ge(out_ready, g + 1)
                sp.dma_start(out_d[:, bass.ds(g * GB, GB), :], rows(g)).then_inc(out_stored, 16)

            spread_leaves(0, True)
            with sp.Fori(0, G - 1) as g:
                spread_leaves(g + 1, False)
                store(g)
            for c in HALVES:
                sp.wait_ge(tail_ready, c.turn)
                b = (G - 1) * GB + c.b0
                sp.dma_start(out_d[:, b:b + c.nb, :], h[:, b:b + c.nb, :]).then_inc(out_stored, 16)
            sp.wait_ge(out_stored, 16 * (G - 1 + len(HALVES)))

        @block.gpsimd
        def _(pool):
            nc.gpsimd.memset(ident[:, :], 0.0).then_inc(ident_zero, 1)
            nc.gpsimd.memset(neg_half[:, :], -0.5).then_inc(neg_half_set, 1)
            pool.wait_ge(ident_zero, 1)
            nc.gpsimd.affine_select(out=ident[:, :], in_=ident[:, :], compare_op=ALU.not_equal, fill=1.0,
                                    base=0, pattern=[[-1, P]], channel_multiplier=1).then_inc(ident_ready, 1)

            def gather(b, done):
                nc.gpsimd.indirect_dma_start(
                    out=h[:, b, :], out_offset=None, in_=tok_w,
                    in_offset=bass.IndirectOffsetOnAxis(ap=ids_cols[:, b:b + 1], axis=0)).then_inc(done, 16)

            def inverse_deviation(k, turn, part):
                pool.wait_ge(ln_var[k], turn)
                nc.gpsimd.tensor_tensor(rstd[k][:, part], veps[k][:, part], neg_half[:, part],
                                        ALU.pow).then_inc(ln_rstd[k], 1)

            def weights_low(e):
                pool.wait_ge(w_hi_done, e + 1)
                nc.gpsimd.tensor_tensor(w1_lo[:, e, :], w1_raw[:, e, :], w1_hi[:, e, :].bitcast(f32), ALU.subtract)
                nc.gpsimd.tensor_tensor(w2_lo[:, e, :, :], w2_raw[:, e, :, :], w2_hi[:, e, :, :].bitcast(f32),
                                        ALU.subtract).then_inc(w_lo_done, 1)

            def add(g, e):
                pool.wait_ge(mixed, g * E + e + 1)
                if e > 1:
                    pool.wait_ge(added, g * (E - 1) + e - 1)
                nc.gpsimd.tensor_tensor(acc[:, :], acc[:, :], part[:, e % 2, :], ALU.add).then_inc(added, 1)

            pool.wait_ge(ids_turned, 1)
            pool.wait_ge(neg_half_set, 1)
            for c in HALVES:
                for b in range(c.b0, c.b0 + c.nb):
                    gather(b, gathered[c.turn - 1])
            for b in (GB, GB + 1):
                gather(b, gathered_rest)
            for c in HALVES:
                inverse_deviation(0, c.turn, batch_rows(c))
            for b in range(GB + 2, NB):
                gather(b, gathered_rest)
            weights_low(0)
            for c in HALVES:
                inverse_deviation(1, c.turn, batch_rows(c))
            for e in range(1, 4):
                weights_low(e)
            inverse_deviation(0, len(HALVES) + 1, slice(GB, NB))
            for e in range(4, E):
                weights_low(e)

            def slots(g, n, ss, attention):
                for s in ss:
                    if attention and s == 9:
                        inverse_deviation(1, last_turn(n), slice(0, GB))
                    if s % 2 == 0 and s > 2:
                        add(g, s // 2 - 1)

            with pool.Fori(0, G - 1) as g:
                slots(g, g + 1, range(2, U), True)
                add(g, E - 1)
            slots(G - 1, G, range(2, U), False)

        @block.scalar
        def _(act):
            act.dma_start(lam[:, 0:1], log_lambda.rearrange("(a n) -> a n", a=1).to_broadcast([P, 1])).then_inc(lambda_in, 16)
            act.wait_ge(lambda_in, 16)
            nc.scalar.activation(lam[:, 1:2], lam[:, 0:1], ACT.Exp).then_inc(lam_exp, 1)

            def turned(c):
                act.wait_ge(xn_turned, c.turn)
                nc.scalar.activation(xn_t[:, tokens(c)], c.banks[0][:, 0:c.nb * S], ACT.Copy).then_inc(xn_t_ready, 1)

            def values(c):
                act.wait_ge(v_done, c.turn)
                nc.scalar.activation(v[:, batch_rows(c), 0:D], c.banks[1][:, 0:c.nb * D].rearrange("p (b d) -> p b d", b=c.nb),
                                     ACT.Copy).then_inc(v_ready, 1)

            def queries_keys(c):
                act.wait_ge(qk_done, c.turn)
                nc.scalar.activation(qk[:, batch_rows(c), :, 0:HD],
                                     c.banks[0][:, 0:c.nb * 2 * HD].rearrange("p (b j c) -> p b j c", b=c.nb, j=2),
                                     ACT.Copy).then_inc(qk_ready, 1)

            def queries(c):
                act.wait_ge(qk_turned, c.turn)
                nc.scalar.activation(q_t[:, tokens(c)], c.banks[0][0:AUG, 0:c.nb * S], ACT.Copy).then_inc(q_t_ready, 1)

            def softmax(c):
                act.wait_ge(dist_ready, c.turn)
                nc.scalar.activation(prob[:, batch_rows(c), :], dist[:, batch_rows(c), :], ACT.Exp,
                                     scale=neg_s).then_inc(prob_ready, 1)

            def expert_input(c):
                act.wait_ge(x_turned, c.turn)
                nc.scalar.activation(x_t[:, tokens(c)], c.banks[1][:, 0:c.nb * S], ACT.Copy).then_inc(x_t_ready, 1)

            def input_high(c, first=False):
                act.wait_ge(x_turned, c.turn)
                if not first:
                    act.wait_ge(up_done, c.group * U * UT)
                nc.scalar.activation(x_hi[:, tokens(c)], c.banks[1][:, 0:c.nb * S], ACT.Copy).then_inc(x_hi_ready, 1)

            def weights_high(e):
                act.wait_ge(weights_in[e], 32)
                nc.scalar.activation(w1_hi[:, e, :], w1_raw[:, e, :], ACT.Copy)
                nc.scalar.activation(w2_hi[:, e, :, :], w2_raw[:, e, :, :], ACT.Copy).then_inc(w_hi_done, 1)

            def router_tanh(n):
                act.wait_ge(z_ready, n + 1)
                nc.scalar.activation(th[:, :, :], z[:, :, :], ACT.Tanh, scale=0.5).then_inc(th_ready, 1)

            def leaves_turned(n):
                act.wait_ge(leaf_turned, n + 1)
                nc.scalar.activation(leaf_t[:, :], pa[0][0:E, :], ACT.Copy).then_inc(leaf_t_ready, 1)

            def gelu(g, u, first=False):
                e, kp = u // UPE, u % UPE
                for t in range(UT):
                    act.wait_ge(up_done, (g * U + u) * UT + t + 1)
                    if t == 0 and (not first or u >= 2):
                        act.wait_ge(g_lo_done, g * U + u - 1)
                    last = nc.scalar.activation(g_full[:, u % 2, t * N:(t + 1) * N],
                                                hid[u % 2][:, t * N:(t + 1) * N], ACT.Gelu,
                                                bias=b1_t(e, kp * UT + t))
                last.then_inc(gelu_done, 1)
                if hi_on_act(u):
                    act.wait_ge(gelu_done, g * U + u + 1)
                    if not first or u >= HS:
                        act.wait_ge(down_done, g * U + u - HS + 1)
                    nc.scalar.activation(g_hi[:, u % HS, :], g_full[:, u % 2, :], ACT.Copy).then_inc(g_hi_act, 1)

            for stages, experts in (((turned,), (0,)), ((queries_keys, values), (1,)), ((queries,), (2,))):
                for c in HALVES:
                    for stage in stages:
                        stage(c)
                for e in experts:
                    weights_high(e)
            act.wait_ge(lam_step, 4)
            for c in HALVES:
                softmax(c)
            nc.scalar.activation(warm[:, :], lam[:, 1:2], ACT.Gelu)
            for e in range(3, E):
                weights_high(e)
            for c in HALVES:
                input_high(c, True)
            for c in HALVES:
                expert_input(c)
            gelu(0, 0, True)
            gelu(0, 1, True)
            router_tanh(0)

            def slots(g, n, ss, attention, first):
                for s in ss:
                    c = whole(n) if attention else None
                    if attention and s == 4:
                        turned(c)
                    if attention and s == 6:
                        queries(c)
                    if attention and s == 12:
                        expert_input(c)
                    if attention and s == 13:
                        router_tanh(n)
                        input_high(c)
                    if s + 2 < U:
                        gelu(g, s + 2, first)
                    elif attention:
                        gelu(n, s + 2 - U)
                    if first and s == 0:
                        leaves_turned(0)
                    if attention and s == 4:
                        queries_keys(c)
                        values(c)
                    if attention and s == 7:
                        softmax(c)
                    if attention and s == 14:
                        leaves_turned(n)

            slots(0, 1, range(0, 2), False, True)
            with act.Fori(0, G - 1) as g:
                slots(g, g + 1, range(2, U), True, False)
                slots(g + 1, g + 2, range(0, 2), False, False)
            slots(G - 1, G, range(2, U), False, False)

        @block.vector
        def _(dve):
            dve.memset(ids_rows[:, :], 0).then_inc(ids_cleared, 1)
            dve.memset(qk[:, :, 0, HD + 1:HD + 2], 1.0)
            dve.memset(qk[:, :, 1, HD:HD + 1], 1.0)
            dve.memset(v[:, :, D:D + 1], 1.0)
            dve.wait_ge(ids_in, 16)
            for j in range(S // 32):
                last = dve.transpose(ids_cols[32 * j:32 * j + 32, :], ids_rows[:, 32 * j:32 * j + 32])
            last.then_inc(ids_turned, 1)

            def moments(k, turn, b0, nb, row):
                for b in range(b0, b0 + nb):
                    last = dve.bn_stats(stats[k][:, b, :], row(b))
                last.then_inc(ln_stats[k], 1)
                dve.wait_ge(gathered[0], 16 * GB // 2)
                dve.wait_ge(ln_stats[k], turn)
                for b in range(b0, b0 + nb):
                    last = dve.bn_aggr(moment[k][:, b, :], stats[k][:, b, :])
                last.then_inc(ln_moments[k], 1)
                part = slice(b0, b0 + nb)
                dve.wait_ge(ln_moments[k], turn)
                dve.tensor_scalar(veps[k][:, part], moment[k][:, part, 1], LN_EPS, None, ALU.add).then_inc(ln_var[k], 1)

            def row_of(c, b):
                return h[:, bass.ds(c.group * GB + b, 1), :].rearrange("p a d -> p (a d)")

            def normalize(k, c):
                for b in range(c.b0, c.b0 + c.nb):
                    at = bass.ds(c.group * GB + b, 1) if k == 0 else slice(b, b + 1)
                    last = dve.tensor_scalar(xn[:, b, :], row_of(c, b), moment[k][:, at, 0], rstd[k][:, at],
                                             ALU.subtract, ALU.mult)
                last.then_inc(ln_done[k], 1)

            def norms(c):
                bs = batch_rows(c)
                dve.wait_ge(qk_ready, c.turn)
                for j, scale in ((0, 1.0), (1, 0.25)):
                    last = dve.scalar_tensor_tensor(out=sq[:, bs, j, :], in0=qk[:, bs, j, 0:HD], scalar=scale,
                                                    in1=qk[:, bs, j, 0:HD], op0=ALU.mult, op1=ALU.mult)
                last.then_inc(sq_done, 1)
                dve.wait_ge(sq_done, c.turn)
                for j in range(2):
                    last = dve.tensor_reduce(qk[:, bs, j, HD + j:HD + j + 1], sq[:, bs, j, :], AX.X, ALU.add)
                last.then_inc(norms_done, 1)

            def keys(c):
                dve.wait_ge(qk_turned, c.turn)
                dve.tensor_copy(k_t[:, tokens(c)], c.banks[1][0:AUG, 0:c.nb * S]).then_inc(k_t_ready, 1)

            def distances(c):
                bs = batch_rows(c)
                d = c.banks[0][:, 0:c.nb * S].rearrange("p (b m) -> p b m", b=c.nb)
                dve.wait_ge(cross_done, c.turn)
                dve.tensor_reduce(dmin[:, bs], d, AX.X, ALU.min).then_inc(dmin_ready, 1)
                dve.wait_ge(dmin_ready, c.turn)
                dve.tensor_scalar(dclip[:, bs], dmin[:, bs], 0.0, None, ALU.max).then_inc(dclip_ready, 1)
                dve.wait_ge(dclip_ready, c.turn)
                dve.scalar_tensor_tensor(out=dist[:, bs, :], in0=d, scalar=0.0,
                                         in1=dclip[:, bs].unsqueeze(2).to_broadcast([P, c.nb, S]),
                                         op0=ALU.max, op1=ALU.subtract).then_inc(dist_ready, 1)

            def probs_turned(c):
                dve.wait_ge(prob_turned, c.turn)
                dve.tensor_copy(prob_t[:, tokens(c)], c.banks[1][:, 0:c.nb * S]).then_inc(prob_t_ready, 1)

            def attend(c):
                dve.wait_ge(pv_done, c.turn)
                per_bank = c.nb // 2
                for j in range(2):
                    sums = c.banks[j][:, 0:per_bank * (D + 1)].rearrange("p (b d) -> p b d", b=per_bank)[:, :, D]
                    b = c.b0 + j * per_bank
                    last = dve.reciprocal(rinv[:, b:b + per_bank], sums)
                last.then_inc(rinv_ready, 1)
                dve.wait_ge(rinv_ready, c.turn)
                for i in range(c.nb):
                    b = c.b0 + i
                    last = dve.scalar_tensor_tensor(out=row_of(c, b), in0=attended(c, i)[:, 0:D],
                                                    scalar=rinv[:, b:b + 1], in1=row_of(c, b), op0=ALU.mult, op1=ALU.add)
                last.then_inc(h_ready, 1)

            def expert_moments(c):
                dve.wait_ge(gathered[0], 16 * GB // 2)
                dve.wait_ge(h_ready, c.turn)
                moments(1, c.turn, c.b0, c.nb, lambda b: row_of(c, b))

            def expert_normalize(c):
                dve.wait_ge(ln_rstd[1], c.turn)
                normalize(1, c)

            def input_low(c):
                dve.wait_ge(x_hi_ready, c.turn)
                dve.wait_ge(x_t_ready, c.turn)
                dve.tensor_tensor(x_lo[:, tokens(c)], x_t[:, tokens(c)], x_hi[:, tokens(c)].bitcast(f32),
                                  ALU.subtract).then_inc(x_lo_ready, 1)

            def router_bias(n):
                dve.wait_ge(router_done, n + 1)
                src = pa[0][:, 0:GB * 8].rearrange("p (b c) -> p b c", b=GB)[:, :, 0:NODES]
                dve.tensor_tensor(z[:, :, :], src, rb_bc[:, :].unsqueeze(1).to_broadcast([P, GB, NODES]),
                                  ALU.add).then_inc(z_ready, 1)

            def leaves(n):
                dve.wait_ge(th_ready, n + 1)
                dve.tensor_scalar(side[:, :, :, 0], th[:, :, :], -0.5, 0.5, ALU.mult, ALU.add)
                dve.tensor_scalar(side[:, :, :, 1], th[:, :, :], 0.5, 0.5, ALU.mult, ALU.add).then_inc(side_ready, 1)
                dve.wait_ge(side_ready, n + 1)
                dve.tensor_tensor(leaf2[:, :, :, :], side[:, :, 0, :].unsqueeze(3).to_broadcast([P, GB, 2, 2]),
                                  side[:, :, 1:3, :], ALU.mult).then_inc(leaf2_ready, 1)
                dve.wait_ge(leaf2_ready, n + 1)
                dve.tensor_tensor(leaf3[:, :, :, :],
                                  leaf2[:, :, :, :].rearrange("p b i j -> p b (i j)").unsqueeze(3).to_broadcast([P, GB, 4, 2]),
                                  side[:, :, 3:7, :], ALU.mult).then_inc(leaf3_ready, 1)

            def split(g, u, first=False):
                if not hi_on_act(u):
                    dve.wait_ge(gelu_done, g * U + u + 1)
                    if not first or u >= HS:
                        dve.wait_ge(down_done, g * U + u - HS + 1)
                    dve.tensor_copy(g_hi[:, u % HS, :], g_full[:, u % 2, :]).then_inc(g_hi_dve, 1)
                wait_high(dve, g, u)
                dve.tensor_tensor(g_lo[:, u % HS, :], g_full[:, u % 2, :], g_hi[:, u % HS, :].bitcast(f32),
                                  ALU.subtract).then_inc(g_lo_done, 1)

            def mix(g, e):
                dve.wait_ge(down_done, g * U + UPE * (e + 1))
                if e == 0:
                    dve.wait_ge(leaf_first, 16 * g + 16)
                if e == E // 2:
                    dve.wait_ge(leaf_second, 16 * g + 16)
                if e > 2:
                    dve.wait_ge(added, g * (E - 1) + e - 2)
                dst = acc[:, :] if e == 0 else part[:, e % 2, :]
                dve.scalar_tensor_tensor(out=dst, in0=y[e % 2][:, :], scalar=b2_t(e), in1=leaf_bc[:, e, :],
                                         op0=ALU.add, op1=ALU.mult).then_inc(mixed, 1)

            def finish(g):
                dve.wait_ge(acc_turned, g + 1)
                dve.tensor_tensor(rows(g), pa[1][:, :].rearrange("p (b d) -> p b d", b=GB), rows(g),
                                  ALU.add).then_inc(out_ready, 1)

            dve.wait_ge(rows_turned, 1)
            wt = pa[0][:, 0:2 * HD + D]
            dve.tensor_copy(wqkv_t[:, 0:HD], wt[:, 0:HD])
            dve.tensor_scalar(wqkv_t[:, HD:2 * HD], wt[:, HD:2 * HD], -2.0, None, ALU.mult)
            dve.tensor_copy(wqkv_t[:, 2 * HD:], wt[:, 2 * HD:]).then_inc(proj_ready, 1)
            dve.tensor_copy(small_t[:, :], pa[0][:, 2 * P:2 * P + ROWS]).then_inc(small_ready, 1)
            dve.wait_ge(lam_exp, 1)
            dve.tensor_scalar(lam[:, 2:3], lam[:, 1:2], LAM_MIN, 2.0 ** 0.5, ALU.max, ALU.mult).then_inc(lam_step, 1)
            dve.wait_ge(lam_step, 1)
            dve.tensor_tensor(lam[:, 3:4], lam[:, 2:3], lam[:, 2:3], ALU.mult).then_inc(lam_step, 1)
            dve.wait_ge(lam_step, 2)
            dve.reciprocal(lam[:, 5:6], lam[:, 3:4]).then_inc(lam_step, 1)
            dve.wait_ge(lam_step, 3)
            dve.tensor_scalar(lam[:, 4:5], lam[:, 5:6], -1.0, None, ALU.mult).then_inc(lam_step, 1)

            def attention_moments(c):
                dve.wait_ge(gathered[c.turn - 1], 16 * c.nb)
                moments(0, c.turn, c.b0, c.nb, lambda b: h[:, b, :])

            def attention_normalize(c):
                dve.wait_ge(ln_rstd[0], c.turn)
                normalize(0, c)

            for stage in (attention_moments, attention_normalize, norms, keys, distances):
                for c in HALVES:
                    stage(c)
            for stage in (probs_turned, attend, expert_moments, expert_normalize, input_low):
                for c in HALVES:
                    stage(c)
            dve.wait_ge(gathered_rest, 16 * (NB - GB))
            moments(0, len(HALVES) + 1, GB, NB - GB, lambda b: h[:, b, :])
            dve.wait_ge(bias_in, 16)
            split(0, 0, True)
            router_bias(0)
            leaves(0)
            split(0, 1, True)

            def slots(g, n, ss, attention, first):
                for s in ss:
                    c = whole(n) if attention else None
                    if attention and s == 2:
                        dve.wait_ge(ln_rstd[0], len(HALVES) + 1)
                        normalize(0, c)
                    if s % 2 == 0 and s > 0:
                        mix(g, s // 2 - 1)
                    if s == 0 and not first:
                        mix(g - 1, E - 1)
                    if attention:
                        if s == 5:
                            norms(c)
                        if s == 6:
                            keys(c)
                        if s == 7:
                            distances(c)
                        if s == 8:
                            probs_turned(c)
                        if s == 9:
                            attend(c)
                            expert_moments(c)
                        if s == 10:
                            expert_normalize(c)
                        if s == 13:
                            router_bias(n)
                            leaves(n)
                            input_low(c)
                    if s + 2 < U:
                        split(g, s + 2, first)
                    elif attention:
                        split(n, s + 2 - U)
                    if s == 1 and not first:
                        finish(g - 1)

            slots(0, 1, range(0, 2), False, True)
            with dve.Fori(0, G - 1) as g:
                slots(g, g + 1, range(2, U), True, False)
                slots(g + 1, g + 2, range(0, 2), False, False)
            slots(G - 1, G, range(2, U), False, False)
            g, e = G - 1, E - 1
            dve.wait_ge(down_done, g * U + UPE * (e + 1))
            dve.wait_ge(added, g * (E - 1) + e - 2)
            for c in HALVES:
                dve.scalar_tensor_tensor(out=part[:, e % 2, tokens(c)], in0=y[e % 2][:, tokens(c)], scalar=b2_t(e),
                                         in1=leaf_bc[:, e, tokens(c)], op0=ALU.add, op1=ALU.mult).then_inc(tail_mixed, 1)
            dve.wait_ge(added, G * (E - 1) - 1)
            for c in HALVES:
                dve.wait_ge(tail_mixed, c.turn)
                dve.tensor_tensor(acc[:, tokens(c)], acc[:, tokens(c)], part[:, e % 2, tokens(c)],
                                  ALU.add).then_inc(tail_added, 1)
            for i, c in enumerate(HALVES):
                dve.wait_ge(tail_turned, c.turn)
                rows_c = h[:, g * GB + c.b0:g * GB + c.b0 + c.nb, :]
                dve.tensor_tensor(rows_c, pa[i][:, 0:c.nb * D].rearrange("p (b d) -> p b d", b=c.nb), rows_c,
                                  ALU.add).then_inc(tail_ready, 1)

        @block.tensor
        def _(pe):
            mm, turn = nc.tensor.matmul, nc.tensor.transpose
            pe.wait_ge(ident_ready, 1)
            pe.wait_ge(rows_in, 16 * 6)
            turn(pa[0][:, 0:P], wqk_rows[:, :], ident[:, :])
            turn(pa[0][:, P:2 * P], wv_rows[:, :], ident[:, :])
            turn(pa[0][:, 2 * P:2 * P + ROWS], small_rows[0:ROWS, :], ident[0:ROWS, 0:ROWS]).then_inc(rows_turned, 1)

            def norm_turn(k, c):
                pe.wait_ge(ln_done[k], c.turn)
                for i in range(c.nb):
                    last = turn(c.banks[k][:, i * P:(i + 1) * P], xn[:, c.b0 + i, :], ident[:, :])
                last.then_inc((xn_turned, x_turned)[k], 1)

            def project(c):
                pe.wait_ge(xn_t_ready, c.turn)
                for weights, bank, done in ((wqkv_t[:, 0:2 * HD], c.banks[0], qk_done),
                                            (wqkv_t[:, 2 * HD:], c.banks[1], v_done)):
                    for i in range(c.nb):
                        x_b = xn_t[:, (c.b0 + i) * P:(c.b0 + i + 1) * P]
                        last = mm(bank[:, i * P:(i + 1) * P], x_b, weights, start=True, stop=True)
                    last.then_inc(done, 1)

            def qk_turn(c):
                pe.wait_ge(v_ready, c.turn)
                pe.wait_ge(norms_done, c.turn)
                for j in range(2):
                    for i in range(c.nb):
                        last = turn(c.banks[j][0:AUG, i * P:(i + 1) * P], qk[:, c.b0 + i, j, :], ident[:, :])
                last.then_inc(qk_turned, 1)

            def distances(c):
                pe.wait_ge(q_t_ready, c.turn)
                pe.wait_ge(k_t_ready, c.turn)
                for i in range(c.nb):
                    tok = slice((c.b0 + i) * P, (c.b0 + i + 1) * P)
                    last = mm(c.banks[0][:, i * P:(i + 1) * P], q_t[:, tok], k_t[:, tok], start=True, stop=True)
                last.then_inc(cross_done, 1)

            def probs_turn(c):
                pe.wait_ge(prob_ready, c.turn)
                for i in range(c.nb):
                    last = turn(c.banks[1][:, i * P:(i + 1) * P], prob[:, c.b0 + i, :], ident[:, :])
                last.then_inc(prob_turned, 1)

            def attend(c):
                pe.wait_ge(prob_t_ready, c.turn)
                for i in range(c.nb):
                    b = c.b0 + i
                    last = mm(attended(c, i), prob_t[:, b * P:(b + 1) * P], v[:, b, :], start=True, stop=True)
                last.then_inc(pv_done, 1)

            def router(n):
                pe.wait_ge(x_t_ready, last_turn(n))
                for b in range(GB):
                    last = mm(pa[0][:, 8 * b:8 * b + NODES], x_t[:, b * P:(b + 1) * P], rw_t, start=True, stop=True)
                last.then_inc(router_done, 1)

            def leaf_turn(n):
                pe.wait_ge(leaf3_ready, n + 1)
                for b in range(GB):
                    last = turn(pa[0][0:E, b * P:(b + 1) * P], leaf3[:, b, :, :].rearrange("p i j -> p (i j)"), ident[:, :])
                last.then_inc(leaf_turned, 1)

            def up(g, u, first=False):
                e, kp = u // UPE, u % UPE
                if kp == 0:
                    pe.wait_ge(w_hi_done, e + 1)
                    pe.wait_ge(w_lo_done, e + 1)
                if u == 0:
                    pe.wait_ge(x_hi_ready, last_turn(g))
                if not first or u >= 2:
                    pe.wait_ge(gelu_done, g * U + u - 1)
                for t in range(UT):
                    k = kp * UT + t
                    dst = hid[u % 2][:, t * N:(t + 1) * N]
                    w_hi, w_lo = w1_hi[:, e, k * P:(k + 1) * P], w1_lo[:, e, k * P:(k + 1) * P]
                    mm(dst, w_hi, x_hi[:, :], start=True, stop=False)
                    mm(dst, w_lo, x_hi[:, :], start=False, stop=False)
                    if u == 0 and t == 0:
                        pe.wait_ge(x_lo_ready, last_turn(g))
                    mm(dst, w_hi, x_lo[:, :], start=False, stop=True).then_inc(up_done, 1)

            def down(g, u, first=False):
                e, kp = u // UPE, u % UPE
                dst = y[e % 2][:, :]
                wait_high(pe, g, u)
                if kp == 0 and e != 1 and (not first or e >= 2):
                    pe.wait_ge(mixed, g * E + e - 1)
                for t in range(UT):
                    k = kp * UT + t
                    mm(dst, w2_hi[:, e, k, :], g_hi[:, u % HS, t * N:(t + 1) * N], start=k == 0, stop=False)
                    mm(dst, w2_lo[:, e, k, :], g_hi[:, u % HS, t * N:(t + 1) * N], start=False, stop=False)
                pe.wait_ge(g_lo_done, g * U + u + 1)
                for t in range(UT):
                    k = kp * UT + t
                    last = mm(dst, w2_hi[:, e, k, :], g_lo[:, u % HS, t * N:(t + 1) * N], start=False, stop=k == KT - 1)
                last.then_inc(down_done, 1)

            def sum_turn(g):
                pe.wait_ge(added, (g + 1) * (E - 1))
                for b in range(GB):
                    last = turn(pa[1][:, b * P:(b + 1) * P], acc[:, b * P:(b + 1) * P], ident[:, :])
                last.then_inc(acc_turned, 1)

            pe.wait_ge(small_ready, 1)
            for c in HALVES:
                norm_turn(0, c)
            pe.wait_ge(proj_ready, 1)
            for stage in (project, qk_turn, distances, probs_turn, attend):
                for c in HALVES:
                    stage(c)
            for c in HALVES:
                norm_turn(1, c)
            up(0, 0, True)
            up(0, 1, True)
            router(0)

            def slots(g, n, ss, attention, first):
                for s in ss:
                    if s == U - 2:
                        down(g, s, first)
                    if s + 2 < U:
                        up(g, s + 2, first)
                    elif attention:
                        up(n, s + 2 - U)
                    c = whole(n) if attention else None
                    if attention:
                        if s == 4:
                            project(c)
                        if s == 9:
                            attend(c)
                        if s == 14:
                            leaf_turn(n)
                    if s != U - 2:
                        down(g, s, first)
                    if first and s == 0:
                        leaf_turn(0)
                    if s == 1 and not first:
                        sum_turn(g - 1)
                    if attention:
                        if s == 3:
                            norm_turn(0, c)
                        if s == 5:
                            qk_turn(c)
                        if s == 6:
                            distances(c)
                        if s == 8:
                            probs_turn(c)
                        if s == 11:
                            norm_turn(1, c)
                        if s == 12:
                            router(n)

            slots(0, 1, range(0, 2), False, True)
            with pe.Fori(0, G - 1) as g:
                slots(g, g + 1, range(2, U), True, False)
                slots(g + 1, g + 2, range(0, 2), False, False)
            slots(G - 1, G, range(2, U), False, False)
            for i, c in enumerate(HALVES):
                pe.wait_ge(tail_added, c.turn)
                for b in range(c.nb):
                    at = (c.b0 + b) * P
                    last = turn(pa[i][:, b * P:(b + 1) * P], acc[:, at:at + P], ident[:, :])
                last.then_inc(tail_turned, 1)


_INS = ['x', 'L0_tok_w', 'L0_attn_Wq', 'L0_attn_Wk', 'L0_attn_Wv', 'L0_attn_log_lambda',
        'L0_ffn_rw', 'L0_ffn_rb', 'L0_ffn_w1', 'L0_ffn_b1', 'L0_ffn_w2', 'L0_ffn_b2']
_OUTS = [((16, 128, 128), 'float32')]


def kernel(**inputs):
    import numpy as _np
    import concourse.bacc as _bacc
    from concourse import mybir as _mybir
    from concourse.bass_utils import run_bass_kernel_spmd as _run

    nc = _bacc.Bacc("TRN2", target_bir_lowering=False, num_devices=1)
    arrays, args = {}, []
    for name in _INS:
        a = _np.ascontiguousarray(inputs[name])
        arrays[f"in_{name}_dram"] = a
        args.append(nc.dram_tensor(f"in_{name}_dram", a.shape, _mybir.dt.from_np(a.dtype), kind="ExternalInput").ap())
    for i, (shape, dtype) in enumerate(_OUTS):
        dt = _mybir.dt.from_np(_np.dtype(dtype))
        args.append(nc.dram_tensor(f"out_{i}_dram", shape, dt, kind="ExternalOutput").ap())
    bass_lm_tower_kernel(nc, *args)
    r = _run(nc, [arrays], core_ids=[0])
    got = tuple(r.results[0][f"out_{i}_dram"] for i in range(len(_OUTS)))
    return got[0]
```
